# Optimizing a Trainium2 kernel written in Bass

```python
import numpy as np
import jax
import jax.numpy as jnp

def _softmax(x, axis=-1):
    return jax.nn.softmax(x, axis=axis)

def _gelu(x):
    return jax.nn.gelu(x, approximate=True)

def _silu(x):
    return jax.nn.silu(x)

def _sigmoid(x):
    return jax.nn.sigmoid(x)

def _layernorm(x, axis=-1, eps=1e-05):
    m = jnp.mean(x, axis=axis, keepdims=True)
    v = jnp.var(x, axis=axis, keepdims=True)
    return (x - m) / jnp.sqrt(v + eps)

def _scatter_add(tgt, idx, src, axis=0):
    return tgt.at[idx].add(src)

def _segment_sum(src, seg, n):
    return jax.ops.segment_sum(src, seg, n)
kernel_name = 'mk_gnn_preln_d1_gnn_r8_5bf8d1'

def setup_inputs(seed: int=0):
    np.random.seed(seed)
    _w = jnp.asarray

    def _rec_inputs():
        import jax
        import jax.numpy as jnp
        _gk = jax.random.key(seed)
        x = -0.000202 + 1 * jax.random.normal(jax.random.fold_in(_gk, 1), (12500, 128), jnp.float32)
        src = jax.random.randint(jax.random.fold_in(_gk, 2), (400000,), 0, 12500, jnp.int32)
        dst = jnp.minimum((12500 * jax.random.uniform(jax.random.fold_in(_gk, 3), (400000,)) ** 2.0).astype(jnp.int32), 99999)
        _o = jnp.argsort(dst, stable=True)
        src = src[_o]
        dst = dst[_o]
        edge_attr_64 = 0.000155561 + 1.00019 * jax.random.normal(jax.random.fold_in(_gk, 11), (400000, 64), jnp.float32)
        return (x, src, dst, edge_attr_64)
    x, src, dst, edge_attr_64 = _rec_inputs()

    def _L0_gnn_setup():
        import jax, jax.numpy as jnp
        import numpy as np
        N_NODES, N_EDGES = (6250, 75000)
        NODE_DIM, EDGE_DIM = (128, 64)
        H, HD = (4, 32)
        key = jax.random.key(seed)
        k = jax.random.split(key, 6)
        node_features = jax.random.normal(k[0], (N_NODES, NODE_DIM), jnp.float32)
        edge_indices = jax.random.randint(k[1], (2, N_EDGES), 0, N_NODES, jnp.int32)
        edge_features = jax.random.normal(k[2], (N_EDGES, EDGE_DIM), jnp.float32)
        W_node = jax.random.normal(k[3], (H * HD, NODE_DIM), jnp.float32) / np.sqrt(NODE_DIM).astype(np.float32)
        W_edge = jax.random.normal(k[4], (H * HD, EDGE_DIM), jnp.float32) / np.sqrt(EDGE_DIM).astype(np.float32)
        a = jax.random.normal(k[5], (H, 3 * HD), jnp.float32)
        return {'node_features': node_features, 'edge_indices': edge_indices, 'edge_features': edge_features, 'W_node': W_node, 'W_edge': W_edge, 'a': a}
    _L0_gnn_all = _L0_gnn_setup()
    _L0_gnn_in = {k: v for k, v in _L0_gnn_all.items() if k in ('W_node', 'W_edge', 'a')}
    del _L0_gnn_all
    return {'x': x, 'src': src, 'dst': dst, 'edge_attr_64': edge_attr_64, 'L0_gnn_W_node': _L0_gnn_in['W_node'], 'L0_gnn_W_edge': _L0_gnn_in['W_edge'], 'L0_gnn_a': _L0_gnn_in['a']}

def reference(x, src, dst, edge_attr_64, L0_gnn_W_node, L0_gnn_W_edge, L0_gnn_a):
    import jax
    import jax.numpy as jnp

    def _L0_gnn_ref(node_features, edge_indices, edge_features, W_node, W_edge, a):
        import jax, jax.numpy as jnp
        import numpy as np
        N_NODES, N_EDGES = (6250, 75000)
        NODE_DIM, EDGE_DIM = (128, 64)
        H, HD = (4, 32)
        num_nodes = node_features.shape[0]
        num_edges = edge_indices.shape[1]
        h = (node_features @ W_node.T).reshape(num_nodes, H, HD)
        e = (edge_features @ W_edge.T).reshape(num_edges, H, HD)
        src, tgt = (edge_indices[0], edge_indices[1])
        h_src = h[src]
        h_tgt = h[tgt]
        att_in = jnp.concatenate([h_src, h_tgt, e], axis=-1)
        att = jnp.sum(att_in * a, axis=-1)
        att = jnp.where(att > 0, att, 0.2 * att)
        m = jnp.maximum(jax.ops.segment_max(att, tgt, num_segments=num_nodes), 0.0)
        ex = jnp.exp(att - m[tgt])
        ones = jnp.ones((num_edges,), node_features.dtype)
        deg = jax.ops.segment_sum(ones, tgt, num_segments=num_nodes)
        denom = jax.ops.segment_sum(ex, tgt, num_segments=num_nodes) + (num_edges - deg)[:, None] * jnp.exp(-m)
        w = ex / denom[tgt]
        h_prime = jax.ops.segment_sum(w[:, :, None] * h_src, tgt, num_segments=num_nodes)
        return h_prime.reshape(num_nodes, H * HD)
    edge_index = jnp.stack([src, dst])
    h = jnp.maximum(_layernorm(x, axis=-1), 0.0)
    x = x + _L0_gnn_ref(h, edge_index, edge_attr_64, L0_gnn_W_node, L0_gnn_W_edge, L0_gnn_a)
    return x

_drawn_inputs = setup_inputs


def setup_inputs(seed=0):
    import zlib

    import numpy as np

    out = dict(_drawn_inputs(seed))
    spreads = {}
    factors = {}
    for name, (base, spread) in spreads.items():
        noise = np.random.default_rng([zlib.crc32(name.encode()), seed]).standard_normal(out[name].shape)
        drawn = base * np.exp(spread * noise) if base else spread * noise
        out[name] = jnp.asarray(drawn.astype(out[name].dtype))
    for name, factor in factors.items():
        out[name] = (out[name] * factor).astype(out[name].dtype)
    return out
```

```python
from contextlib import ExitStack

import concourse.bass as bass
from concourse import mybir

F32 = mybir.dt.float32
I32 = mybir.dt.int32
ALU = mybir.AluOpType
ACT = mybir.ActivationFunctionType
AX_X = mybir.AxisListType.X

P = 128

CHUNK = 25
SLOTS = CHUNK + 1
GROUP = 7
OUT_GROUP = 14
PROBES = 10
EPS = 1e-5
SLOPE = 0.2


def gnn_kernel(nc, x, src, dst_runs, dst, run_heads, run_edges, feats, w_node, w_node_t, w_edge, a_cols, out):
    E, N, D = dst.shape[0] * dst.shape[1], out.shape[0], out.shape[1]
    H = 4
    HD = D // H
    FE = w_edge.shape[1]
    RUN = E // P
    T = RUN // CHUNK
    PAIRS = SLOTS // 2
    KT = N // P
    HW = HD + 1
    W = H * HW
    RW = W + H
    HEADS, HEAD = run_heads.shape[1], dst.shape[1]
    assert RUN == T * CHUNK and T % 2 == 1 and N == KT * P and KT % (2 * GROUP) == 0

    table = nc.dram_tensor("table", (N, W), F32).ap()
    tgt_table = nc.dram_tensor("tgt_table", (N, H), F32).ap()
    dst_f = nc.dram_tensor("dst_f", (HEADS, HEAD), F32).ap()
    first_edge = nc.dram_tensor("first_edge", (N, 1), I32).ap()
    seeds = nc.dram_tensor("seeds", (E + N, H), F32).ap()
    running = nc.dram_tensor("running", (E + P, RW), F32).ap()
    table_v = table.rearrange("(p k) w -> p k w", p=P)
    tgt_table_v = tgt_table.rearrange("(p k) h -> p (k h)", p=P)
    first_edge_v = first_edge.rearrange("(p k) o -> p (k o)", p=P)
    dst_f_v = dst_f.rearrange("a b -> (a b)").rearrange("(p c) -> p c", p=P)
    dst_v = dst.rearrange("a b -> (a b)").rearrange("(p c) -> p c", p=P)
    seeds_v = seeds[0:E, :].rearrange("(p c) h -> p (c h)", p=P)
    running_v = running[0:E, :].rearrange("(p c) w -> p (c w)", p=P)
    x_v = x.rearrange("(p k) d -> p (k d)", p=P)
    out_v = out.rearrange("(p k) d -> p (k d)", p=P)

    with ExitStack() as ctx:
        def sb(name, shape, dt=F32):
            return ctx.enter_context(nc.sbuf_tensor(name, shape, dt))

        def sem(name):
            return ctx.enter_context(nc.semaphore(name))

        wn = sb("wn", [P, D])
        we2 = sb("we2", [P, 2, FE])
        ac = sb("ac", [P, 3])
        ab = sb("ab", [P, 3, H])
        wc = sb("wc", [P, RW])
        wscore = sb("wscore", [P, 2, H])
        ident = sb("ident", [P, P])
        ones = sb("ones", [P, P])
        node_i = sb("node_i", [P, KT + 2], I32)
        node_id = sb("node_id", [P, KT + 2])
        heads_i = sb("heads_i", [P, HEADS], I32)
        heads_f = sb("heads_f", [P, HEADS])
        junk = sb("junk", [P, HEADS])
        junk2 = sb("junk2", [P, HEAD])
        piece = sb("piece", [P, 2, PROBES])
        piece_i = sb("piece_i", [P, 2, PROBES], I32)
        below = sb("below", [P, 2, PROBES])
        fe = sb("fe", [P, KT + 2])
        fe_i = sb("fe_i", [P, KT], I32)
        deg = sb("deg", [P, KT])
        some = sb("some", [P, KT])
        none_n = sb("none_n", [P, KT])
        spare = sb("spare", [P, KT])
        seed_at = sb("seed_at", [P, KT])
        last_at = sb("last_at", [P, KT])
        tgt_all = sb("tgt_all", [P, KT, H])
        seed_idx = sb("seed_idx", [P, 2, GROUP], I32)
        seed_val = sb("seed_val", [P, 2, GROUP, H])
        last_idx = sb("last_idx", [P, 2, OUT_GROUP], I32)
        xg = sb("xg", [P, 2, GROUP, D])
        st = sb("st", [P, GROUP, 6])
        mv = sb("mv", [P, GROUP, 2])
        var = sb("var", [P, GROUP])
        dev = sb("dev", [P, GROUP])
        rstd = sb("rstd", [P, GROUP])
        ht = sb("ht", [P, GROUP * D])
        tab = sb("tab", [P, 2, GROUP, RW])
        re_i = sb("re_i", [P, 5], I32)
        re = sb("re", [P, 5])
        cont = sb("cont", [P, 1])
        tail_id = sb("tail_id", [P, 1])
        bt = sb("bt", [P, 4])
        rep = sb("rep", [P, 1])
        diag = sb("diag", [P, H, P])
        same = sb("same", [P, P])
        tail_next_i = sb("tail_next_i", [P, 1], I32)
        tail_end_i = sb("tail_end_i", [P, 1], I32)
        tail_end = sb("tail_end", [P, 1])
        tail_last_i = sb("tail_last_i", [P, 1], I32)
        tail_put = sb("tail_put", [P, 1])
        tail_put_i = sb("tail_put_i", [P, 1], I32)
        run_seed = sb("run_seed", [P, H])
        src_c = sb("src_c", [P, 2, CHUNK], I32)
        dst_c = sb("dst_c", [P, 2, SLOTS], I32)
        seed_c = sb("seed_c", [P, 2, CHUNK, H])
        feat_c = sb("feat_c", [P, 2, PAIRS, P])
        rows = sb("rows", [P, 2, CHUNK, W])
        keep = sb("keep", [P, H, SLOTS])
        seed_s = sb("seed_s", [P, H, SLOTS])
        tgt_s = sb("tgt_s", [P, H, SLOTS])
        att = sb("att", [P, H, CHUNK])
        att_s = sb("att_s", [P, H, SLOTS])
        top = sb("top", [P, 2, H, SLOTS])
        expo = sb("expo", [P, 2, H, CHUNK])
        expd = sb("expd", [P, 2, H, CHUNK])
        fade = sb("fade", [P, 2, H, SLOTS])
        fade_w = sb("fade_w", [P, 2, H, HW, SLOTS])
        terms = sb("terms", [P, H, HW, SLOTS])
        sums = sb("sums", [P, 2, H, HW, SLOTS])
        dump = sb("dump", [P, 2, CHUNK, RW])
        probe_rows = [dump[:, :, :, :].rearrange("p b c w -> p (b c w)")[:, 0:PROBES * HEAD].rearrange("p (i e) -> p i e", e=HEAD),
                      sums[:, :, :, :, :].rearrange("p b h w s -> p (b h w s)")[:, 0:PROBES * HEAD].rearrange("p (i e) -> p i e", e=HEAD)]
        zeros = fade_w[:, :, :, :, :].rearrange("p b h w s -> p (b h w s)")[:, 0:RUN * H // 2]
        dst_all = rows[:, :, :, :].rearrange("p b c w -> p (b c w)")[:, 0:RUN].bitcast(I32)
        dst_all_f = terms[:, :, :, :].rearrange("p h w s -> p (h w s)")[:, 0:RUN]
        def as_groups(buffer, width):
            return buffer[:, 0:2 * OUT_GROUP * width].rearrange("p (b k w) -> p b k w", b=2, k=OUT_GROUP)

        fin_rows = as_groups(dump[:, :, :, :].rearrange("p b c w -> p (b c w)"), RW)
        x_g = as_groups(rows[:, :, :, :].rearrange("p b c w -> p (b c w)"), D)
        y_g = as_groups(fade_w[:, :, :, :, :].rearrange("p b h w s -> p (b h w s)"), D)
        d1 = sb("d1", [P, OUT_GROUP, H])
        d2 = sb("d2", [P, OUT_GROUP, H])
        fin_top = sb("fin_top", [P, OUT_GROUP, H])
        run_spare_i = sb("run_spare_i", [P, 1], I32)
        run_spare = sb("run_spare", [P, 1])
        gmax = sb("gmax", [P, H])
        gd = sb("gd", [P, 2, H])
        ge = sb("ge", [P, 2, H])
        mask4 = sb("mask4", [P, H, P])
        tail_row = sb("tail_row", [P, RW])
        tail_s = sb("tail_s", [P, H, HW])
        merged = sb("merged", [P, RW])

        banks = ctx.enter_context(nc.psum_tensor("banks", [P, 8, 512], F32))

        def pair(name):
            return [sem(f"{name}{b}") for b in range(2)]

        dst_in, heads_in, weights_in, edges_in = sem("dst_in"), sem("heads_in"), sem("weights_in"), sem("edges_in")
        dst_float, dst_f_out, zeros_set, seeds_zeroed = sem("dst_float"), sem("dst_f_out"), sem("zeros_set"), sem("seeds_zeroed")
        node_iota, ident_zero, ident_set, ones_set, ids_ready = sem("node_iota"), sem("ident_zero"), sem("ident_set"), sem("ones_set"), sem("ids_ready")
        cleared, spread_a, vectors, weights_ready = sem("cleared"), sem("spread_a"), sem("vectors"), sem("weights_ready")
        located, pool_past, dve_past = sem("located"), sem("pool_past"), sem("dve_past")
        counted, pieces, piece_ready, probe_in, probed = sem("counted"), sem("pieces"), sem("piece_ready"), pair("probe_in"), sem("probed")
        x_in, x_stats, x_aggr, x_var, x_dev, x_rstd, x_normed = pair("x_in"), sem("x_stats"), sem("x_aggr"), sem("x_var"), sem("x_dev"), sem("x_rstd"), sem("x_normed")
        transposed, ht_ready, projected, tab_ready, table_out, tgt_kept = pair("transposed"), sem("ht_ready"), sem("projected"), sem("tab_ready"), pair("table_out"), sem("tgt_kept")
        tgt_out, node_step, nodes_placed, first_out = sem("tgt_out"), sem("node_step"), sem("nodes_placed"), sem("first_out")
        edge_step, tail_diag, tail_spread, same_ready, tail_ready, tail_end_in, tail_step = (
            sem("edge_step"), sem("tail_diag"), sem("tail_spread"), sem("same_ready"), sem("tail_ready"), sem("tail_end_in"), sem("tail_step"))
        run_seed_in, staged, seed_out, seeds_ready = sem("run_seed_in"), sem("staged"), pair("seed_out"), sem("seeds_ready")
        src_in, dstc_in, seed_in, feat_in, rows_in = pair("src_in"), pair("dstc_in"), pair("seed_in"), pair("feat_in"), pair("rows_in")
        carries, scores_ready, kept, seeded, tgt_filled, added, scored, leaked, floored, topped = (
            sem("carries"), sem("scores_ready"), sem("kept"), sem("seeded"), sem("tgt_filled"), sem("added"), sem("scored"), sem("leaked"),
            sem("floored"), sem("topped"))
        faded, expo_ready, exps_ready, fade_ready, fade_wide, carried, terms_ready, summed = (
            sem("faded"), sem("expo_ready"), sem("exps_ready"), sem("fade_ready"), sem("fade_wide"), sem("carried"), sem("terms_ready"),
            sem("summed"))
        dump_ready, dumped = sem("dump_ready"), pair("dumped")
        gmax_diag, gmax_spread, tail_max, tail_scale, tail_scaled, tail_sums, tail_row_in, merged_ready, merged_out = (
            sem("gmax_diag"), sem("gmax_spread"), sem("tail_max"), sem("tail_scale"), sem("tail_scaled"), sem("tail_sums"),
            sem("tail_row_in"), sem("merged_ready"), sem("merged_out"))
        last_staged, fin_in, xg_in, fin_step, fin_exp_in, fin_exp, fin_free, y_ready, y_out = (
            sem("last_staged"), pair("fin_in"), pair("xg_in"), sem("fin_step"), sem("fin_exp_in"), sem("fin_exp"), sem("fin_free"),
            sem("y_ready"), pair("y_out"))

        block = ctx.enter_context(nc.Block())

        def at_least(eng, s, value):
            if not (isinstance(value, int) and value <= 0):
                eng.wait_ge(s, value)

        def pairwise(eng, n, step, lagging=None, lag=1):
            def both(t, b, before):
                step(t, b, before)
                if lagging and not (isinstance(t, int) and t < lag):
                    if lag == 1:
                        lagging(t - 1, 1 - b, before if b else before - 1)
                    else:
                        lagging(t - 2, b, before - 1)

            peeled = 2 + n % 2
            for t in range(peeled):
                both(t, t % 2, t // 2)
            with eng.Fori(0, (n - peeled) // 2) as j:
                for i in range(2):
                    both(peeled + 2 * j + i, (peeled + i) % 2, (peeled + i) // 2 + j)
            if lagging:
                for t in range(n - lag, n):
                    lagging(t, t % 2, t // 2)

        NG = KT // GROUP
        NS = (KT + 2) // PROBES
        NO = KT // OUT_GROUP
        assert NG % 2 == 0 and NS % 2 == 0 and NO % 2 == 1 and NS * PROBES == KT + 2


        @block.sync
        def _(sp):
            sp.dma_start(dst_all, dst_v).then_inc(dst_in, 16)
            sp.dma_start(heads_i[:, :], run_heads).then_inc(heads_in, 16)
            sp.dma_start(wn[:, :], w_node).then_inc(weights_in, 16)
            sp.dma_start(wc[:, 0:W].rearrange("p (h w) -> p h w", h=H)[:, :, 0:HD],
                         w_node_t.rearrange("p (h w) -> p h w", h=H)).then_inc(weights_in, 16)
            for half in range(2):
                sp.dma_start(we2[:, half, :], w_edge).then_inc(weights_in, 16)
            sp.dma_start(ac[:, :], a_cols).then_inc(weights_in, 16)
            sp.dma_start(re_i[:, :], run_edges).then_inc(edges_in, 16)
            sp.wait_ge(dst_float, 1)
            sp.dma_start(dst_f_v, dst_all_f).then_inc(dst_f_out, 16)
            sp.wait_ge(zeros_set, 1)
            for half in range(2):
                sp.dma_start(seeds_v[:, half * (RUN * H // 2):(half + 1) * (RUN * H // 2)], zeros).then_inc(seeds_zeroed, 16)

            def load_x(g, b, before):
                at_least(sp, transposed[b], before)
                sp.dma_start(xg[:, b, :, :], x_v[:, bass.ds(g * (GROUP * D), GROUP * D)].rearrange("p (k d) -> p k d", k=GROUP)).then_inc(x_in[b], 16)

            def store_rows(g, b, before):
                sp.wait_ge(tab_ready, g + 1)
                sp.dma_start(table_v[:, bass.ds(g * GROUP, GROUP), :], tab[:, b, :, 0:W]).then_inc(table_out[b], 16)

            pairwise(sp, NG, load_x, store_rows, lag=2)
            sp.wait_ge(tgt_kept, NG)
            sp.dma_start(tgt_table_v, tgt_all[:, :, :].rearrange("p k h -> p (k h)")).then_inc(tgt_out, 16)
            sp.wait_ge(nodes_placed, 1)
            sp.dma_start(first_edge_v, fe_i[:, :]).then_inc(first_out, 16)
            sp.wait_ge(run_seed_in, 16)
            for b in range(2):
                sp.wait_ge(seed_out[b], 16 * GROUP * NG // 2)
            sp.dma_start(seeds_v[:, 0:H], run_seed[:, :]).then_inc(seeds_ready, 16)
            sp.wait_ge(seeds_ready, 16)

            def store_running(t, b, before):
                sp.wait_ge(dump_ready, t + 1)
                sp.dma_start(running_v[:, bass.ds(t * (CHUNK * RW), CHUNK * RW)],
                             dump[:, b, :, :].rearrange("p c w -> p (c w)")).then_inc(dumped[b], 16)

            def load_chunk(t, b, before):
                at_least(sp, terms_ready, t - 1)
                sp.dma_start(src_c[:, b, :], src[:, bass.ds(t * CHUNK, CHUNK)]).then_inc(src_in[b], 16)
                sp.dma_start(dst_c[:, b, :], dst_runs[:, bass.ds(t * CHUNK, SLOTS)]).then_inc(dstc_in[b], 16)
                sp.dma_start(seed_c[:, b, :, :], seeds_v[:, bass.ds(t * (CHUNK * H), CHUNK * H)].rearrange("p (c h) -> p c h", h=H)).then_inc(seed_in[b], 16)
                sp.dma_start(feat_c[:, b, :, :].rearrange("p i e -> p (i e)"), feats[bass.ds(t * P, P), :]).then_inc(feat_in[b], 16)

            pairwise(sp, T, load_chunk, store_running, lag=2)

            def load_x_again(g, b, before):
                at_least(sp, y_ready, g - 1)
                sp.dma_start(x_g[:, b, :, :], x_v[:, bass.ds(g * (OUT_GROUP * D), OUT_GROUP * D)].rearrange("p (k d) -> p k d", k=OUT_GROUP)).then_inc(xg_in[b], 16)

            def store_y(g, b, before):
                sp.wait_ge(y_ready, g + 1)
                sp.dma_start(out_v[:, bass.ds(g * (OUT_GROUP * D), OUT_GROUP * D)], y_g[:, b, :, :].rearrange("p k d -> p (k d)")).then_inc(y_out[b], 16)

            sp.wait_ge(terms_ready, T)
            pairwise(sp, NO, load_x_again, store_y, lag=2)
            sp.wait_ge(y_out[0], 16 * ((NO + 1) // 2))
            sp.wait_ge(y_out[1], 16 * (NO // 2))

        @block.gpsimd
        def _(pool):
            def gather(to, rows_of, idx):
                return pool.indirect_dma_start(to, None, rows_of, bass.IndirectOffsetOnAxis(ap=idx, axis=0))

            def scatter(rows_of, idx, values):
                return pool.indirect_dma_start(rows_of, bass.IndirectOffsetOnAxis(ap=idx, axis=0), values, None)

            pool.iota(node_i[:, :], pattern=[[1, KT + 2]], base=0, channel_multiplier=KT).then_inc(node_iota, 1)
            pool.iota(run_spare_i[:, :], pattern=[[0, 1]], base=E, channel_multiplier=1).then_inc(node_iota, 1)
            pool.memset(ident[:, :], 0.0).then_inc(ident_zero, 1)
            pool.memset(ones[:, :], 1.0).then_inc(ones_set, 1)
            pool.wait_ge(ident_zero, 1)
            pool.affine_select(out=ident[:, :], in_=ident[:, :], compare_op=ALU.not_equal, fill=1.0, base=0,
                               pattern=[[-1, P]], channel_multiplier=1).then_inc(ident_set, 1)
            pool.wait_ge(dst_f_out, 16)

            def probe(s, b, before):
                pool.wait_ge(piece_ready, s + 1)
                pool.sem_inc(pool_past, 1)
                for i in range(PROBES):
                    gather(probe_rows[b][:, i, :], dst_f, piece_i[:, b, i:i + 1]).then_inc(probe_in[b], 16)

            pairwise(pool, NS, probe)
            pool.wait_ge(edges_in, 16)
            pool.wait_ge(tgt_out, 16)
            gather(run_seed[:, :], tgt_table, re_i[:, 0:1]).then_inc(run_seed_in, 16)
            pool.wait_ge(seeds_zeroed, 32)

            def scatter_seeds(g, b, before):
                pool.wait_ge(staged, 2 * g + 2)
                pool.sem_inc(pool_past, 1)
                for i in range(GROUP):
                    scatter(seeds, seed_idx[:, b, i:i + 1], seed_val[:, b, i, :]).then_inc(seed_out[b], 16)

            pairwise(pool, NG, scatter_seeds)
            pool.wait_ge(first_out, 16)
            pool.wait_ge(tail_ready, 1)
            gather(tail_end_i[:, :], first_edge, tail_next_i[:, :]).then_inc(tail_end_in, 16)

            for b in range(2):
                pool.wait_ge(table_out[b], 16 * NG // 2)

            def gather_chunk(t, b, before):
                pool.wait_ge(src_in[b], 16 * (before + 1))
                pool.sem_inc(pool_past, 1)
                for c in range(CHUNK):
                    gather(rows[:, b, c, :], table, src_c[:, b, c:c + 1]).then_inc(rows_in[b], 16)

            pairwise(pool, T, gather_chunk)

            pool.wait_ge(dumped[0], 16 * ((T + 1) // 2))
            pool.wait_ge(dumped[1], 16 * (T // 2))
            pool.wait_ge(tail_step, 3)
            gather(tail_row[:, :], running[0:E, :], tail_last_i[:, :]).then_inc(tail_row_in, 16)
            pool.wait_ge(merged_ready, 1)
            scatter(running, tail_put_i[:, :], merged[:, :]).then_inc(merged_out, 16)
            pool.wait_ge(merged_out, 16)

            def gather_last(g, b, before):
                pool.wait_ge(last_staged, g + 1)
                at_least(pool, y_ready, g - 1)
                pool.sem_inc(pool_past, 1)
                for i in range(OUT_GROUP):
                    gather(fin_rows[:, b, i, :], running[0:E, :], last_idx[:, b, i:i + 1]).then_inc(fin_in[b], 16)

            pairwise(pool, NO, gather_last)

        @block.tensor
        def _(pe):
            pe.wait_ge(weights_in, 16 * 5)
            pe.wait_ge(spread_a, H)
            pe.matmul(banks[:, 7, 0:2 * H], wn[:, :], ab[:, 0:2, :].rearrange("p j h -> p (j h)"), start=True, stop=True).then_inc(vectors, 1)
            pe.matmul(banks[:, 7, 2 * H:3 * H], we2[:, :, :].rearrange("p a f -> p (a f)"), ab[:, 2, :], start=True, stop=True).then_inc(vectors, 1)
            pe.wait_ge(tail_diag, 1)
            pe.wait_ge(ones_set, 1)
            pe.matmul(banks[:, 6, 0:P], ones[:, :], diag[:, 0, :], start=True, stop=True).then_inc(tail_spread, 1)

            pe.wait_ge(ident_set, 1)
            pe.wait_ge(weights_ready, 3)
            pe.wait_ge(same_ready, 1)

            def project(g, b, before):
                pe.wait_ge(x_normed, g + 1)
                at_least(pe, ht_ready, 2 * g)
                for i in range(GROUP):
                    last = pe.transpose(banks[:, 2 * b + i // 4, (i % 4) * P:(i % 4 + 1) * P], xg[:, b, i, :], ident[:, :])
                last.then_inc(transposed[b], 1)
                pe.wait_ge(ht_ready, 2 * g + 2)
                at_least(pe, tab_ready, g)
                for i in range(GROUP):
                    last = pe.matmul(banks[:, 4 + i // 2, (i % 2) * RW:(i % 2 + 1) * RW], ht[:, i * P:(i + 1) * P], wc[:, :],
                                     start=True, stop=True)
                last.then_inc(projected, 1)

            pairwise(pe, NG, project)
            pe.wait_ge(tab_ready, NG)

            def score_chunk(t, b, before):
                pe.wait_ge(feat_in[b], 16 * (before + 1))
                for i in range(PAIRS):
                    last = pe.matmul(banks[:, b, i * 2 * H:(i + 1) * 2 * H], feat_c[:, b, i, :],
                                     wscore[:, :, :].rearrange("p a h -> p (a h)"), start=True, stop=True)
                last.then_inc(scores_ready, 1)

            pairwise(pe, T, score_chunk)

            pe.wait_ge(gmax_diag, 1)
            pe.matmul(banks[:, 2, :], ones[:, :], diag[:, :, :].rearrange("p h q -> p (h q)"), start=True, stop=True).then_inc(gmax_spread, 1)
            pe.wait_ge(tail_scaled, 1)
            pe.matmul(banks[:, 3, 0:W], same[:, :], tail_s[:, :, :].rearrange("p h w -> p (h w)"), start=True, stop=True).then_inc(tail_sums, 1)

        @block.scalar
        def _(act):
            act.wait_ge(dst_in, 16)
            act.activation(dst_all_f, dst_all, ACT.Copy).then_inc(dst_float, 1)

            def deviation(g, b, before):
                act.wait_ge(x_var, g + 1)
                act.activation(dev[:, :], var[:, :], ACT.Sqrt).then_inc(x_dev, 1)

            def relu(g, b, before):
                act.wait_ge(transposed[b], before + 1)
                at_least(act, projected, g)
                flat = banks[:, 2 * b:2 * b + 2, :].rearrange("p a n -> p (a n)")
                act.activation(ht[:, 0:4 * P], flat[:, 0:4 * P], ACT.Relu).then_inc(ht_ready, 1)
                act.activation(ht[:, 4 * P:GROUP * P], flat[:, 4 * P:GROUP * P], ACT.Relu).then_inc(ht_ready, 1)

            pairwise(act, NG, deviation, relu)

            act.wait_ge(nodes_placed, 3)
            act.wait_ge(tgt_kept, NG)

            def stage_seeds(g, b, before):
                at_least(act, seed_out[b], 16 * GROUP * before)
                act.activation(seed_idx[:, b, :], seed_at[:, bass.ds(g * GROUP, GROUP)], ACT.Copy).then_inc(staged, 1)
                act.activation(seed_val[:, b, :, :], tgt_all[:, bass.ds(g * GROUP, GROUP), :], ACT.Copy).then_inc(staged, 1)

            pairwise(act, NG, stage_seeds)

            def exps(t, b):
                act.wait_ge(expo_ready, t + 1)
                act.activation(expd[:, :, :, :], expo[:, :, :, :], ACT.Exp).then_inc(exps_ready, 1)

            def widen(t, b):
                act.wait_ge(fade_ready, t + 1)
                at_least(act, summed, t - 1)
                act.activation(fade_w[:, b, :, :, :], fade[:, b, :, None, :].to_broadcast([P, H, HW, SLOTS]), ACT.Copy).then_inc(fade_wide, 1)

            def carry(t, b):
                act.wait_ge(summed, t)
                act.activation(terms[:, :, :, 0], sums[:, 1 - b, :, :, CHUNK], ACT.Copy).then_inc(carried, 1)

            def empty(t, b, before):
                act.wait_ge(summed, t + 1)
                at_least(act, dumped[b], 16 * before)
                act.activation(dump[:, b, :, 0:W].rearrange("p c (h w) -> p h w c", h=H), sums[:, b, :, :, 1:SLOTS], ACT.Copy)
                act.activation(dump[:, b, :, W:RW].rearrange("p c h -> p h c"), top[:, b, :, 1:SLOTS], ACT.Copy).then_inc(dump_ready, 1)

            def weights(t, b, before):
                exps(t, b)
                widen(t, b)
                if not (isinstance(t, int) and t == 0):
                    carry(t, b)

            pairwise(act, T, weights, empty)

            act.wait_ge(tail_max, 1)
            act.activation(ge[:, :, :], gd[:, :, :], ACT.Exp).then_inc(tail_scale, 1)

            def stage_last(g, b, before):
                at_least(act, fin_in[b], 16 * OUT_GROUP * before)
                act.activation(last_idx[:, b, :], last_at[:, bass.ds(g * OUT_GROUP, OUT_GROUP)], ACT.Copy).then_inc(last_staged, 1)

            def fin_exps(g, b, before):
                act.wait_ge(fin_exp_in, g + 1)
                act.activation(d1[:, :, :], fin_top[:, :, :], ACT.Exp, scale=-1.0).then_inc(fin_exp, 1)

            pairwise(act, NO, stage_last, fin_exps)

        @block.vector
        def _(dve):
            dve.wait_ge(heads_in, 16)
            dve.tensor_copy(heads_f[:, :], heads_i[:, :]).then_inc(ids_ready, 1)
            dve.wait_ge(node_iota, 2)
            dve.tensor_copy(run_spare[:, :], run_spare_i[:, :])
            dve.tensor_copy(node_id[:, :], node_i[:, :]).then_inc(ids_ready, 1)
            dve.memset(ab[:, :, :], 0.0).then_inc(cleared, 1)
            dve.memset(wscore[:, :, :], 0.0).then_inc(cleared, 1)
            dve.memset(zeros, 0.0).then_inc(zeros_set, 1)
            dve.wait_ge(ids_ready, 2)

            def find_piece(s, b, before):
                at_least(dve, located, s - 1)
                for i in range(PROBES):
                    at_least(dve, counted, s * PROBES + i)
                    dve.tensor_scalar(junk[:, :], heads_f[:, :], node_id[:, bass.ds(s * PROBES + i, 1)], None, ALU.is_lt, ALU.add,
                                      accum_out=piece[:, b, i:i + 1]).then_inc(counted, 1)
                dve.wait_ge(counted, (s + 1) * PROBES)
                dve.tensor_scalar(piece[:, b, :], piece[:, b, :], -1.0, 0.0, ALU.add, ALU.max).then_inc(pieces, 1)
                dve.wait_ge(pieces, s + 1)
                dve.tensor_copy(piece_i[:, b, :], piece[:, b, :]).then_inc(piece_ready, 1)

            def count_piece(s, b, before):
                dve.wait_ge(probe_in[b], 16 * PROBES * (before + 1))
                for i in range(PROBES):
                    at_least(dve, probed, s * PROBES + i)
                    dve.tensor_scalar(junk2[:, :], probe_rows[b][:, i, :], node_id[:, bass.ds(s * PROBES + i, 1)], None, ALU.is_lt,
                                      ALU.add, accum_out=below[:, b, i:i + 1]).then_inc(probed, 1)
                dve.wait_ge(probed, (s + 1) * PROBES)
                dve.scalar_tensor_tensor(fe[:, bass.ds(s * PROBES, PROBES)], piece[:, b, :], float(HEAD), below[:, b, :], ALU.mult, ALU.add).then_inc(located, 1)

            pairwise(dve, NS, find_piece, count_piece)

            dve.wait_ge(cleared, 2)
            dve.wait_ge(weights_in, 16 * 5)
            for h in range(H):
                dve.tensor_copy(ab[HD * h:HD * (h + 1), :, h], ac[HD * h:HD * (h + 1), :]).then_inc(spread_a, 1)
            dve.wait_ge(vectors, 2)
            dve.tensor_copy(wc[:, 0:W].rearrange("p (h w) -> p h w", h=H)[:, :, HD], banks[:, 7, 0:H])
            dve.tensor_copy(wc[:, W:RW], banks[:, 7, H:2 * H]).then_inc(weights_ready, 1)
            for half in range(2):
                dve.tensor_copy(wscore[FE * half:FE * (half + 1), half, :], banks[FE * half:FE * (half + 1), 7, 2 * H:3 * H]).then_inc(weights_ready, 1)

            step = 0

            def link(s, ins):
                nonlocal step
                step += 1
                ins.then_inc(s, 1)
                dve.wait_ge(s, step)

            dve.wait_ge(edges_in, 16)
            link(edge_step, dve.tensor_copy(re[:, :], re_i[:, :]))
            link(edge_step, dve.tensor_tensor(cont[:, :], re[:, 1:2], re[:, 2:3], ALU.is_equal))
            link(edge_step, dve.scalar_tensor_tensor(tail_id[:, :], re[:, 1:2], 1.0, cont[:, :], ALU.add, ALU.mult))
            link(edge_step, dve.tensor_scalar(tail_id[:, :], tail_id[:, :], -1.0, None, ALU.add))
            link(edge_step, dve.tensor_tensor(bt[:, 0:1], re[:, 3:4], re[:, 1:2], ALU.is_equal))
            link(edge_step, dve.tensor_tensor(bt[:, 1:2], re[:, 3:4], re[:, 4:5], ALU.is_equal))
            link(edge_step, dve.tensor_tensor(bt[:, 2:3], bt[:, 0:1], bt[:, 1:2], ALU.mult))
            link(edge_step, dve.tensor_scalar(bt[:, 3:4], bt[:, 2:3], -1.0, 1.0, ALU.mult, ALU.add))
            link(edge_step, dve.tensor_tensor(rep[:, :], bt[:, 3:4], cont[:, :], ALU.mult))
            dve.tensor_scalar(tail_next_i[:, :], re[:, 1:2], 1.0, None, ALU.add).then_inc(tail_ready, 1)
            dve.wait_ge(ident_set, 1)
            dve.tensor_scalar(diag[:, 0, :], ident[:, :], tail_id[:, 0:1], None, ALU.mult).then_inc(tail_diag, 1)
            dve.wait_ge(tail_spread, 1)
            dve.tensor_scalar(same[:, :], banks[:, 6, 0:P], tail_id[:, 0:1], None, ALU.is_equal).then_inc(same_ready, 1)

            def normalize(g, b, before):
                dve.wait_ge(x_in[b], 16 * (before + 1))
                for i in range(GROUP):
                    last = dve.bn_stats(st[:, i, :], xg[:, b, i, :])
                last.then_inc(x_stats, 1)
                dve.wait_ge(x_stats, g + 1)
                dve.sem_inc(dve_past, 1)
                for i in range(GROUP):
                    last = dve.bn_aggr(mv[:, i, :], st[:, i, :])
                last.then_inc(x_aggr, 1)
                dve.wait_ge(x_aggr, g + 1)
                dve.tensor_scalar(var[:, :], mv[:, :, 1], EPS, None, ALU.add).then_inc(x_var, 1)
                dve.wait_ge(x_dev, g + 1)
                dve.reciprocal(rstd[:, :], dev[:, :]).then_inc(x_rstd, 1)
                dve.wait_ge(x_rstd, g + 1)
                for i in range(GROUP):
                    last = dve.tensor_scalar(xg[:, b, i, :], xg[:, b, i, :], mv[:, i, 0:1], rstd[:, i:i + 1], ALU.subtract, ALU.mult)
                last.then_inc(x_normed, 1)

            def take_rows(g, b, before):
                dve.wait_ge(projected, g + 1)
                at_least(dve, table_out[b], 16 * before)
                dve.tensor_copy(tab[:, b, 0:GROUP - 1, :].rearrange("p (a i) w -> p a (i w)", i=2), banks[:, 4:7, 0:2 * RW])
                dve.tensor_copy(tab[:, b, GROUP - 1, :], banks[:, 7, 0:RW]).then_inc(tab_ready, 1)
                dve.wait_ge(tab_ready, g + 1)
                dve.tensor_copy(tgt_all[:, bass.ds(g * GROUP, GROUP), :], tab[:, b, :, W:RW]).then_inc(tgt_kept, 1)

            pairwise(dve, NG, normalize, take_rows)

            step = 0
            link(node_step, dve.tensor_tensor(deg[:, :], fe[:, 1:KT + 1], fe[:, 0:KT], ALU.subtract))
            link(node_step, dve.tensor_scalar(some[:, :], deg[:, :], 0.0, None, ALU.is_gt))
            link(node_step, dve.tensor_scalar(none_n[:, :], deg[:, :], -1.0, float(E), ALU.mult, ALU.add))
            link(node_step, dve.tensor_scalar(spare[:, :], node_id[:, 0:KT], float(E), None, ALU.add))
            link(node_step, dve.tensor_tensor(seed_at[:, :], fe[:, 0:KT], spare[:, :], ALU.subtract))
            link(node_step, dve.tensor_tensor(seed_at[:, :], seed_at[:, :], some[:, :], ALU.mult))
            dve.tensor_copy(fe_i[:, :], fe[:, 0:KT]).then_inc(nodes_placed, 1)
            dve.tensor_tensor(seed_at[:, :], seed_at[:, :], spare[:, :], ALU.add).then_inc(nodes_placed, 1)
            dve.tensor_scalar(last_at[:, :], fe[:, 1:KT + 1], -1.0, 0.0, ALU.add, ALU.max).then_inc(nodes_placed, 1)

            dve.wait_ge(tail_end_in, 16)
            step = 0
            dve.tensor_scalar(tail_last_i[:, :], tail_end_i[:, :], -1.0, None, ALU.add)
            link(tail_step, dve.tensor_scalar(tail_end[:, :], tail_end_i[:, :], -1.0, None, ALU.add))
            link(tail_step, dve.scalar_tensor_tensor(tail_put[:, :], tail_end[:, :], run_spare[:, 0:1], rep[:, :], ALU.subtract, ALU.mult))
            link(tail_step, dve.tensor_tensor(tail_put_i[:, :], tail_put[:, :], run_spare[:, :], ALU.add))

            dve.memset(keep[:, :, 0], 0.0)
            for b in range(2):
                dve.memset(fade[:, b, :, 0], 0.0)
                dve.memset(top[:, b, :, :], 0.0)
            dve.memset(tgt_s[:, :, CHUNK], 0.0)
            dve.memset(terms[:, :, :, 0], 0.0).then_inc(carries, 1)
            dve.wait_ge(carries, 1)

            def scan(dst_ap, factors, plus, combine):
                return dve.tensor_tensor_scan(dst_ap, factors, plus, 0.0, ALU.mult, combine)

            def flat(ap):
                return ap.rearrange("p h s -> p (h s)")

            def flat4(ap):
                return ap.rearrange("p h w s -> p (h w s)")

            def chunk(t, b, before):
                at_least(dve, summed, t)
                dve.wait_ge(dstc_in[b], 16 * (before + 1))
                dve.tensor_tensor(keep[:, :, 1:SLOTS], dst_c[:, b, None, 1:SLOTS].to_broadcast([P, H, CHUNK]),
                                  dst_c[:, b, None, 0:CHUNK].to_broadcast([P, H, CHUNK]), ALU.is_equal).then_inc(kept, 1)
                dve.wait_ge(seed_in[b], 16 * (before + 1))
                dve.tensor_copy(seed_s[:, :, 0], tgt_s[:, :, CHUNK])
                dve.tensor_copy(seed_s[:, :, 1:SLOTS], seed_c[:, b, :, :].rearrange("p c h -> p h c")).then_inc(seeded, 1)
                dve.wait_ge(seeded, t + 1)
                dve.wait_ge(kept, t + 1)
                scan(flat(tgt_s[:, :, :]), flat(keep[:, :, :]), flat(seed_s[:, :, :]), ALU.add).then_inc(tgt_filled, 1)
                dve.wait_ge(tgt_filled, t + 1)
                dve.wait_ge(scores_ready, t + 1)
                dve.tensor_tensor(att[:, :, :], banks[:, b, 0:CHUNK * H].rearrange("p (c h) -> p h c", h=H), tgt_s[:, :, 1:SLOTS], ALU.add).then_inc(added, 1)
                dve.wait_ge(added, t + 1)
                dve.wait_ge(rows_in[b], 16 * CHUNK * (before + 1))
                rows_h = rows[:, b, :, :].rearrange("p c (h w) -> p h w c", h=H)
                dve.tensor_tensor(att[:, :, :], att[:, :, :], rows_h[:, :, HD, :], ALU.add).then_inc(scored, 1)
                dve.wait_ge(scored, t + 1)
                dve.scalar_tensor_tensor(att[:, :, :], att[:, :, :], SLOPE, att[:, :, :], ALU.mult, ALU.max).then_inc(leaked, 1)
                dve.wait_ge(leaked, t + 1)
                dve.tensor_copy(att_s[:, :, 0], top[:, 1 - b, :, CHUNK])
                dve.tensor_scalar(att_s[:, :, 1:SLOTS], att[:, :, :], 0.0, None, ALU.max).then_inc(floored, 1)
                dve.wait_ge(floored, t + 1)
                at_least(dve, dump_ready, t - 1)
                scan(flat(top[:, b, :, :]), flat(keep[:, :, :]), flat(att_s[:, :, :]), ALU.max).then_inc(topped, 1)
                dve.wait_ge(topped, t + 1)
                dve.tensor_tensor(expo[:, 0, :, :], keep[:, :, 1:SLOTS], top[:, b, :, 0:CHUNK], ALU.mult).then_inc(faded, 1)
                dve.tensor_tensor(expo[:, 1, :, :], att[:, :, :], top[:, b, :, 1:SLOTS], ALU.subtract)
                dve.wait_ge(faded, t + 1)
                dve.tensor_tensor(expo[:, 0, :, :], expo[:, 0, :, :], top[:, b, :, 1:SLOTS], ALU.subtract).then_inc(expo_ready, 1)
                dve.memset(rows_h[:, :, HD, :], 1.0)
                dve.wait_ge(exps_ready, t + 1)
                dve.tensor_tensor(fade[:, b, :, 1:SLOTS], expd[:, 0, :, :], keep[:, :, 1:SLOTS], ALU.mult).then_inc(fade_ready, 1)
                at_least(dve, summed, t)
                dve.wait_ge(fade_ready, t + 1)
                dve.tensor_tensor(terms[:, :, :, 1:SLOTS], rows_h, expd[:, 1, :, None, :].to_broadcast([P, H, HW, CHUNK]), ALU.mult).then_inc(terms_ready, 1)
                dve.wait_ge(terms_ready, t + 1)
                dve.wait_ge(fade_wide, t + 1)
                at_least(dve, carried, t)
                at_least(dve, dump_ready, t - 1)
                scan(flat4(sums[:, b, :, :, :]), flat4(fade_w[:, b, :, :, :]), flat4(terms[:, :, :, :]), ALU.add).then_inc(summed, 1)

            pairwise(dve, T, chunk)

            dve.wait_ge(topped, T)
            dve.tensor_tensor(diag[:, :, :], ident[:, None, :].to_broadcast([P, H, P]), top[:, 0, :, CHUNK:SLOTS].to_broadcast([P, H, P]), ALU.mult).then_inc(gmax_diag, 1)
            dve.wait_ge(gmax_spread, 1)
            step = 3
            link(tail_step, dve.tensor_tensor(mask4[:, :, :], banks[:, 2, :].rearrange("p (h q) -> p h q", h=H), same[:, None, :].to_broadcast([P, H, P]), ALU.mult))
            link(tail_step, dve.tensor_reduce(gmax[:, :], mask4[:, :, :], AX_X, ALU.max))
            dve.wait_ge(tail_row_in, 16)
            link(tail_step, dve.tensor_tensor(merged[:, W:RW], gmax[:, :], tail_row[:, W:RW], ALU.max))
            dve.tensor_tensor(gd[:, 0, :], top[:, 0, :, CHUNK], merged[:, W:RW], ALU.subtract)
            dve.tensor_tensor(gd[:, 1, :], tail_row[:, W:RW], merged[:, W:RW], ALU.subtract).then_inc(tail_max, 1)
            dve.wait_ge(tail_scale, 1)
            dve.wait_ge(summed, T)
            dve.tensor_tensor(tail_s[:, :, :], sums[:, 0, :, :, CHUNK], ge[:, 0, :, None].to_broadcast([P, H, HW]), ALU.mult).then_inc(tail_scaled, 1)
            row_h = tail_row[:, 0:W].rearrange("p (h w) -> p h w", h=H)
            link(tail_step, dve.tensor_tensor(row_h, row_h, ge[:, 1, :, None].to_broadcast([P, H, HW]), ALU.mult))
            dve.wait_ge(tail_sums, 1)
            dve.tensor_tensor(merged[:, 0:W], banks[:, 3, 0:W], tail_row[:, 0:W], ALU.add).then_inc(merged_ready, 1)

            def finish(g, b, before):
                dve.wait_ge(fin_in[b], 16 * OUT_GROUP * (before + 1))
                fin_h = fin_rows[:, b, :, 0:W].rearrange("p k (h w) -> p k h w", h=H)
                at = bass.ds(g * OUT_GROUP, OUT_GROUP)
                dve.tensor_copy(fin_top[:, :, :], fin_rows[:, b, :, W:RW]).then_inc(fin_exp_in, 1)
                dve.wait_ge(fin_exp, g + 1)
                dve.tensor_tensor(d2[:, :, :], d1[:, :, :], none_n[:, at, None].to_broadcast([P, OUT_GROUP, H]), ALU.mult).then_inc(fin_step, 1)
                dve.wait_ge(fin_step, 4 * g + 1)
                dve.tensor_tensor(d2[:, :, :], d2[:, :, :], fin_h[:, :, :, HD], ALU.add).then_inc(fin_step, 1)
                dve.wait_ge(fin_step, 4 * g + 2)
                dve.reciprocal(d2[:, :, :], d2[:, :, :]).then_inc(fin_step, 1)
                dve.wait_ge(fin_step, 4 * g + 3)
                dve.tensor_tensor(d2[:, :, :], d2[:, :, :], some[:, at, None].to_broadcast([P, OUT_GROUP, H]), ALU.mult).then_inc(fin_step, 1)
                dve.wait_ge(fin_step, 4 * g + 4)
                at_least(dve, y_out[b], 16 * before)
                y_h = y_g[:, b, :, :].rearrange("p k (h w) -> p k h w", h=H)
                dve.tensor_tensor(y_h, fin_h[:, :, :, 0:HD], d2[:, :, :, None].to_broadcast([P, OUT_GROUP, H, HD]), ALU.mult).then_inc(fin_free, 1)
                dve.wait_ge(fin_free, g + 1)
                dve.wait_ge(xg_in[b], 16 * (before + 1))
                dve.tensor_tensor(y_g[:, b, :, :], y_g[:, b, :, :], x_g[:, b, :, :], ALU.add).then_inc(y_ready, 1)

            pairwise(dve, NO, finish)


def kernel(**inputs):
    import numpy as np
    import concourse.bacc as bacc
    from concourse.bass_utils import run_bass_kernel_spmd

    x, src, dst = (np.asarray(inputs[n]) for n in ("x", "src", "dst"))
    feats = np.asarray(inputs["edge_attr_64"])
    w_node, w_edge, a = (np.asarray(inputs[f"L0_gnn_{n}"]) for n in ("W_node", "W_edge", "a"))
    nodes, d = x.shape
    edges, fe = feats.shape
    run = edges // P
    chunks = run // CHUNK
    heads = edges // 625
    padded = -(-nodes // (2 * GROUP * P)) * (2 * GROUP * P)
    x_rows = np.zeros((padded, d), x.dtype)
    x_rows[:nodes] = x
    dst_runs = np.full((P, run + 1), -1, dst.dtype)
    dst_runs[:, 1:] = dst.reshape(P, run)
    run_edges = np.full((P + 2, 5), -1, dst.dtype)
    run_edges[:P, 0], run_edges[:P, 1] = dst_runs[:, 1], dst_runs[:, -1]
    run_edges[:P - 1, 2:4] = run_edges[1:P, 0:2]
    run_edges[:P - 2, 4] = run_edges[2:P, 0]
    cols = np.zeros((P, chunks, SLOTS, fe), feats.dtype)
    cols[:, :, :CHUNK] = feats.reshape(P, chunks, CHUNK, fe)
    feats_t = cols.reshape(P, chunks, SLOTS // 2, 2, fe).transpose(1, 3, 4, 2, 0).reshape(chunks * 2 * fe, -1)
    n_heads, hd = a.shape[0], a.shape[1] // 3
    arrays = {
        "x": x_rows,
        "src": src.reshape(P, run),
        "dst_runs": dst_runs,
        "dst": dst.reshape(heads, -1),
        "run_heads": np.broadcast_to(dst.reshape(heads, -1)[:, 0], (P, heads)),
        "run_edges": run_edges[:P],
        "feats": feats_t,
        "w_node": w_node,
        "w_node_t": w_node.T,
        "w_edge": w_edge,
        "a_cols": a.reshape(n_heads, 3, hd).transpose(0, 2, 1).reshape(n_heads * hd, 3),
    }
    arrays = {n: np.ascontiguousarray(v) for n, v in arrays.items()}
    nc = bacc.Bacc("TRN2", target_bir_lowering=False, num_devices=1)
    args = {n: nc.dram_tensor(f"in_{n}", v.shape, mybir.dt.from_np(v.dtype), kind="ExternalInput").ap() for n, v in arrays.items()}
    out = nc.dram_tensor("out", (padded, d), F32, kind="ExternalOutput").ap()
    gnn_kernel(nc, **args, out=out)
    r = run_bass_kernel_spmd(nc, [{f"in_{n}": v for n, v in arrays.items()}], core_ids=[0])
    return r.results[0]["out"][:nodes]
```

```python
from contextlib import ExitStack

import concourse.bass as bass
from concourse import mybir

F32 = mybir.dt.float32
BF16 = mybir.dt.bfloat16
I32 = mybir.dt.int32
ALU = mybir.AluOpType
ACT = mybir.ActivationFunctionType
AX_X = mybir.AxisListType.X

P = 128

CHUNK = 25
SLOTS = CHUNK + 1
GROUP = 7
OUT_GROUP = 14
EPS = 1e-5
SLOPE = 0.2
ZERO_PARTS = 10


def gnn_kernel(nc, x, src, dst_runs, dst, heads, run_edges, feats, w_node, w_node_t, w_edge, a_cols, out):
    E, N, D = dst.shape[0] * dst.shape[1], out.shape[0], out.shape[1]
    H = 4
    HD = D // H
    FE = w_edge.shape[1]
    RUN = E // P
    T = RUN // CHUNK
    PAIRS = SLOTS // 2
    KT = N // P
    HW = HD + 1
    W = H * HW
    RW = W + H
    HEADS, HEAD = dst.shape
    QT = HEADS // P
    NG, NO = KT // GROUP, KT // OUT_GROUP
    assert HEADS == QT * P and RUN == T * CHUNK and T % 2 == 1 and N == KT * P and KT % (2 * GROUP) == 0

    table = nc.dram_tensor("table", (N, W), F32).ap()
    tgt_table = nc.dram_tensor("tgt_table", (N, H), F32).ap()
    first_edge = nc.dram_tensor("first_edge", (N, 1), I32).ap()
    seeds = nc.dram_tensor("seeds", (E + N, H), F32).ap()
    running = nc.dram_tensor("running", (E + P, RW), F32).ap()
    table_v = table.rearrange("(p k) w -> p k w", p=P)
    tgt_table_v = tgt_table.rearrange("(p k) h -> p (k h)", p=P)
    first_edge_v = first_edge.rearrange("(p k) o -> p (k o)", p=P)
    seeds_v = seeds[0:E, :].rearrange("(p c) h -> p (c h)", p=P)
    running_v = running[0:E, :].rearrange("(p c) w -> p (c w)", p=P)
    x_v = x.rearrange("(p k) d -> p (k d)", p=P)
    out_v = out.rearrange("(p k) d -> p (k d)", p=P)

    with ExitStack() as ctx:
        def sb(name, shape, dt=F32):
            return ctx.enter_context(nc.sbuf_tensor(name, shape, dt))

        def sem(name):
            return ctx.enter_context(nc.semaphore(name))

        wn = sb("wn", [P, D])
        we2 = sb("we2", [P, 2, FE])
        ac = sb("ac", [P, 3])
        ab = sb("ab", [P, 3, H])
        wc = sb("wc", [P, RW])
        wscore = sb("wscore", [P, 2, H])
        ident = sb("ident", [P, P])
        ones = sb("ones", [P, P])
        node_i = sb("node_i", [P, KT + 1], I32)
        node_id = sb("node_id", [P, KT + 1])
        group_i = sb("group_i", [P, GROUP, P], I32)
        group_id = sb("group_id", [P, GROUP, P])
        heads_i = sb("heads_i", [P, QT], I32)
        head = sb("head", [P, 2, QT])
        past = sb("past", [P, QT, GROUP, P], BF16)
        ones_b = sb("ones_b", [P, 1], BF16)
        signs = sb("signs", [P, 2, HEAD])
        piece = sb("piece", [P, KT])
        piece_i = sb("piece_i", [P, 2, GROUP], I32)
        below = sb("below", [P, KT])
        half_id = sb("half_id", [P, KT])
        fe = sb("fe", [P, KT + 1])
        fe_i = sb("fe_i", [P, KT], I32)
        deg = sb("deg", [P, KT])
        some = sb("some", [P, KT])
        none_n = sb("none_n", [P, KT])
        spare = sb("spare", [P, KT])
        seed_at = sb("seed_at", [P, KT])
        last_at = sb("last_at", [P, KT])
        tgt_all = sb("tgt_all", [P, KT, H])
        seed_idx = sb("seed_idx", [P, 2, GROUP], I32)
        seed_val = sb("seed_val", [P, 2, GROUP, H])
        last_idx = sb("last_idx", [P, 2, OUT_GROUP], I32)
        xn = sb("xn", [P, 2, GROUP, D])
        st = sb("st", [P, GROUP, 6])
        mv = sb("mv", [P, 2, GROUP, 2])
        var = sb("var", [P, GROUP])
        dev = sb("dev", [P, 2, GROUP])
        rstd = sb("rstd", [P, GROUP])
        ht = sb("ht", [P, GROUP * D])
        tab = sb("tab", [P, 2, GROUP, RW])
        re_i = sb("re_i", [P, 5], I32)
        re = sb("re", [P, 5])
        cont = sb("cont", [P, 1])
        tail_id = sb("tail_id", [P, 1])
        bt = sb("bt", [P, 4])
        rep = sb("rep", [P, 1])
        diag = sb("diag", [P, H, P])
        same = sb("same", [P, P])
        tail_next_i = sb("tail_next_i", [P, 1], I32)
        tail_end_i = sb("tail_end_i", [P, 1], I32)
        tail_end = sb("tail_end", [P, 1])
        tail_last_i = sb("tail_last_i", [P, 1], I32)
        tail_put = sb("tail_put", [P, 1])
        tail_put_i = sb("tail_put_i", [P, 1], I32)
        run_seed = sb("run_seed", [P, H])
        src_c = sb("src_c", [P, 2, CHUNK], I32)
        dst_c = sb("dst_c", [P, 2, SLOTS], I32)
        seed_c = sb("seed_c", [P, 2, CHUNK, H])
        feat_c = sb("feat_c", [P, 2, PAIRS, P])
        rows = sb("rows", [P, 2, CHUNK, W])
        keep = sb("keep", [P, H, SLOTS])
        seed_s = sb("seed_s", [P, H, SLOTS])
        tgt_s = sb("tgt_s", [P, H, SLOTS])
        att = sb("att", [P, H, CHUNK])
        att_s = sb("att_s", [P, H, SLOTS])
        top = sb("top", [P, 2, H, SLOTS])
        expo = sb("expo", [P, 2, H, CHUNK])
        expd = sb("expd", [P, 2, H, CHUNK])
        fade = sb("fade", [P, 2, H, SLOTS])
        fade_w = sb("fade_w", [P, 2, H, HW, SLOTS])
        terms = sb("terms", [P, H, HW, SLOTS])
        sums = sb("sums", [P, 2, H, HW, SLOTS])
        dump = sb("dump", [P, 2, CHUNK, RW])
        probe_rows = [dump[:, :, :, :].rearrange("p b c w -> p (b c w)")[:, 0:GROUP * HEAD].rearrange("p (i e) -> p i e", e=HEAD),
                      sums[:, :, :, :, :].rearrange("p b h w s -> p (b h w s)")[:, 0:GROUP * HEAD].rearrange("p (i e) -> p i e", e=HEAD)]
        probe_rows = [r.bitcast(I32) for r in probe_rows]
        zeros = terms[:, :, :, :].rearrange("p h w s -> p (h w s)")[:, 0:RUN * H // ZERO_PARTS]
        x_all = [rows[:, :, :, :].rearrange("p b c w -> p (b c w)")[:, 0:KT * D // 2],
                 fade_w[:, :, :, :, :].rearrange("p b h w s -> p (b h w s)")[:, 0:KT * D // 2]]
        def as_groups(buffer, width):
            return buffer[:, 0:2 * OUT_GROUP * width].rearrange("p (b k w) -> p b k w", b=2, k=OUT_GROUP)

        fin_rows = as_groups(dump[:, :, :, :].rearrange("p b c w -> p (b c w)"), RW)
        x_g = as_groups(rows[:, :, :, :].rearrange("p b c w -> p (b c w)"), D)
        y_g = as_groups(fade_w[:, :, :, :, :].rearrange("p b h w s -> p (b h w s)"), D)
        d1 = sb("d1", [P, OUT_GROUP, H])
        d2 = sb("d2", [P, OUT_GROUP, H])
        fin_top = sb("fin_top", [P, OUT_GROUP, H])
        run_spare_i = sb("run_spare_i", [P, 1], I32)
        run_spare = sb("run_spare", [P, 1])
        gmax = sb("gmax", [P, H])
        gd = sb("gd", [P, 2, H])
        ge = sb("ge", [P, 2, H])
        mask4 = sb("mask4", [P, H, P])
        tail_row = sb("tail_row", [P, RW])
        tail_s = sb("tail_s", [P, H, HW])
        merged = sb("merged", [P, RW])

        banks = ctx.enter_context(nc.psum_tensor("banks", [P, 8, 512], F32))

        def pair(name):
            return [sem(f"{name}{b}") for b in range(2)]

        heads_in, weights_in, edges_in = sem("heads_in"), sem("weights_in"), sem("edges_in")
        zeros_set, seeds_zeroed = sem("zeros_set"), sem("seeds_zeroed")
        node_iota, ident_zero, ident_set, ones_set, ids_ready = sem("node_iota"), sem("ident_zero"), sem("ident_set"), sem("ones_set"), sem("ids_ready")
        cleared, spread_a, vectors, weights_ready = sem("cleared"), sem("spread_a"), sem("vectors"), sem("weights_ready")
        assert ZERO_PARTS < NG
        X_PARTS = [(0, 1), (1, KT // GROUP // 2)]
        x_part = [pair(f"x_part{n}_") for n in range(len(X_PARTS))]
        shifted, held = sem("shifted"), sem("held")
        located, pool_past, dve_past = sem("located"), sem("pool_past"), sem("dve_past")
        heads_moved, compared, pieces_summed, piece_ready, probe_in, probed = sem("heads_moved"), sem("compared"), sem("pieces_summed"), sem("piece_ready"), pair("probe_in"), sem("probed")
        x_stats, x_aggr, x_var, x_dev, x_rstd, x_normed = sem("x_stats"), sem("x_aggr"), sem("x_var"), sem("x_dev"), sem("x_rstd"), sem("x_normed")
        transposed, ht_ready, projected, tab_ready, table_out, tgt_kept = pair("transposed"), sem("ht_ready"), sem("projected"), sem("tab_ready"), pair("table_out"), sem("tgt_kept")
        tgt_out, node_step, nodes_placed, first_out = sem("tgt_out"), sem("node_step"), sem("nodes_placed"), sem("first_out")
        edge_step, tail_diag, tail_spread, same_ready, tail_ready, tail_end_in, tail_step = (
            sem("edge_step"), sem("tail_diag"), sem("tail_spread"), sem("same_ready"), sem("tail_ready"), sem("tail_end_in"), sem("tail_step"))
        run_seed_in, staged, seed_out, seeds_ready = sem("run_seed_in"), sem("staged"), pair("seed_out"), sem("seeds_ready")
        src_in, dstc_in, seed_in, feat_in, rows_in = pair("src_in"), pair("dstc_in"), pair("seed_in"), pair("feat_in"), pair("rows_in")
        carries, scores_ready, kept, seeded, tgt_filled, added, scored, leaked, floored, topped = (
            sem("carries"), sem("scores_ready"), sem("kept"), sem("seeded"), sem("tgt_filled"), sem("added"), sem("scored"), sem("leaked"),
            sem("floored"), sem("topped"))
        faded, expo_ready, exps_ready, fade_ready, fade_wide, carried, terms_ready, summed = (
            sem("faded"), sem("expo_ready"), sem("exps_ready"), sem("fade_ready"), sem("fade_wide"), sem("carried"), sem("terms_ready"),
            sem("summed"))
        dump_ready, dumped = sem("dump_ready"), pair("dumped")
        gmax_diag, gmax_spread, tail_max, tail_scale, tail_scaled, tail_sums, tail_row_in, merged_ready, merged_out = (
            sem("gmax_diag"), sem("gmax_spread"), sem("tail_max"), sem("tail_scale"), sem("tail_scaled"), sem("tail_sums"),
            sem("tail_row_in"), sem("merged_ready"), sem("merged_out"))
        last_staged, fin_in, xg_in, fin_step, fin_exp_in, fin_exp, fin_free, y_ready, y_out = (
            sem("last_staged"), pair("fin_in"), pair("xg_in"), sem("fin_step"), sem("fin_exp_in"), sem("fin_exp"), sem("fin_free"),
            sem("y_ready"), pair("y_out"))

        block = ctx.enter_context(nc.Block())

        def at_least(eng, s, value):
            if not (isinstance(value, int) and value <= 0):
                eng.wait_ge(s, value)

        def pairwise(eng, n, step, lagging=None, lag=1):
            def both(t, b, before):
                step(t, b, before)
                if lagging and not (isinstance(t, int) and t < lag):
                    if lag == 1:
                        lagging(t - 1, 1 - b, before if b else before - 1)
                    else:
                        lagging(t - 2, b, before - 1)

            peeled = 2 + n % 2
            for t in range(peeled):
                both(t, t % 2, t // 2)
            with eng.Fori(0, (n - peeled) // 2) as j:
                for i in range(2):
                    both(peeled + 2 * j + i, (peeled + i) % 2, (peeled + i) // 2 + j)
            if lagging:
                for t in range(n - lag, n):
                    lagging(t, t % 2, t // 2)

        assert NG % 2 == 0 and NO % 2 == 1


        @block.sync
        def _(sp):
            sp.dma_start(heads_i[:, :], heads).then_inc(heads_in, 16)
            sp.dma_start(wn[:, :], w_node).then_inc(weights_in, 16)
            sp.dma_start(wc[:, 0:W].rearrange("p (h w) -> p h w", h=H)[:, :, 0:HD],
                         w_node_t.rearrange("p (h w) -> p h w", h=H)).then_inc(weights_in, 16)
            for half in range(2):
                sp.dma_start(we2[:, half, :], w_edge).then_inc(weights_in, 16)
            sp.dma_start(ac[:, :], a_cols).then_inc(weights_in, 16)
            sp.dma_start(re_i[:, :], run_edges).then_inc(edges_in, 16)
            x_pairs = x_v.rearrange("p (a b n) -> p b a n", b=2, n=GROUP * D)
            x_to = [x_all[b].rearrange("p (a n) -> p a n", n=GROUP * D) for b in range(2)]
            for n, (i, j) in enumerate(X_PARTS):
                for b in range(2):
                    sp.dma_start(x_to[b][:, i:j, :], x_pairs[:, b, i:j, :]).then_inc(x_part[n][b], 16)
            def load_inputs(t, b):
                sp.dma_start(src_c[:, b, :], src[:, bass.ds(t * CHUNK, CHUNK)]).then_inc(src_in[b], 16)
                sp.dma_start(dst_c[:, b, :], dst_runs[:, bass.ds(t * CHUNK, SLOTS)]).then_inc(dstc_in[b], 16)
                sp.dma_start(feat_c[:, b, :, :].rearrange("p i e -> p (i e)"), feats[bass.ds(t * P, P), :]).then_inc(feat_in[b], 16)

            for b in range(2):
                load_inputs(b, b)
            sp.wait_ge(zeros_set, 1)
            with sp.Fori(0, ZERO_PARTS) as j:
                sp.wait_ge(piece_ready, j + (NG - ZERO_PARTS))
                sp.dma_start(seeds_v[:, bass.ds(j * (RUN * H // ZERO_PARTS), RUN * H // ZERO_PARTS)], zeros).then_inc(seeds_zeroed, 16)
            sp.wait_ge(tgt_kept, NG)
            sp.dma_start(tgt_table_v, tgt_all[:, :, :].rearrange("p k h -> p (k h)")).then_inc(tgt_out, 16)
            sp.wait_ge(located, 1)
            sp.dma_start(fe[0:P - 1, KT:KT + 1], fe[1:P, 0:1]).then_inc(shifted, 16)
            sp.wait_ge(nodes_placed, 1)
            sp.dma_start(first_edge_v, fe_i[:, :]).then_inc(first_out, 16)
            sp.wait_ge(run_seed_in, 16)
            for b in range(2):
                sp.wait_ge(seed_out[b], 16 * GROUP * NG // 2)
            sp.dma_start(seeds_v[:, 0:H], run_seed[:, :]).then_inc(seeds_ready, 16)
            sp.wait_ge(seeds_ready, 16)

            def store_running(t, b, before):
                sp.wait_ge(dump_ready, t + 1)
                sp.dma_start(running_v[:, bass.ds(t * (CHUNK * RW), CHUNK * RW)],
                             dump[:, b, :, :].rearrange("p c w -> p (c w)")).then_inc(dumped[b], 16)

            def load_chunk(t, b, before):
                at_least(sp, terms_ready, t - 1)
                if not isinstance(t, int) or t >= 2:
                    load_inputs(t, b)
                sp.dma_start(seed_c[:, b, :, :], seeds_v[:, bass.ds(t * (CHUNK * H), CHUNK * H)].rearrange("p (c h) -> p c h", h=H)).then_inc(seed_in[b], 16)

            pairwise(sp, T, load_chunk, store_running, lag=2)

            def load_x_again(g, b, before):
                at_least(sp, y_ready, g - 1)
                sp.dma_start(x_g[:, b, :, :], x_v[:, bass.ds(g * (OUT_GROUP * D), OUT_GROUP * D)].rearrange("p (k d) -> p k d", k=OUT_GROUP)).then_inc(xg_in[b], 16)

            def store_y(g, b, before):
                sp.wait_ge(y_ready, g + 1)
                sp.dma_start(out_v[:, bass.ds(g * (OUT_GROUP * D), OUT_GROUP * D)], y_g[:, b, :, :].rearrange("p k d -> p (k d)")).then_inc(y_out[b], 16)

            sp.wait_ge(terms_ready, T)
            pairwise(sp, NO, load_x_again, store_y, lag=2)
            sp.wait_ge(y_out[0], 16 * ((NO + 1) // 2))
            sp.wait_ge(y_out[1], 16 * (NO // 2))

        @block.gpsimd
        def _(pool):
            def gather(to, rows_of, idx):
                return pool.indirect_dma_start(to, None, rows_of, bass.IndirectOffsetOnAxis(ap=idx, axis=0))

            def scatter(rows_of, idx, values):
                return pool.indirect_dma_start(rows_of, bass.IndirectOffsetOnAxis(ap=idx, axis=0), values, None)

            pool.iota(node_i[:, :], pattern=[[1, KT + 1]], base=0, channel_multiplier=KT).then_inc(node_iota, 1)
            pool.iota(group_i[:, :, :], pattern=[[1, GROUP], [KT, P]], base=0, channel_multiplier=0).then_inc(node_iota, 1)
            pool.iota(run_spare_i[:, :], pattern=[[0, 1]], base=E, channel_multiplier=1).then_inc(node_iota, 1)
            pool.memset(ident[:, :], 0.0).then_inc(ident_zero, 1)
            pool.memset(ones[:, :], 1.0).then_inc(ones_set, 1)
            pool.wait_ge(ident_zero, 1)
            pool.affine_select(out=ident[:, :], in_=ident[:, :], compare_op=ALU.not_equal, fill=1.0, base=0,
                               pattern=[[-1, P]], channel_multiplier=1).then_inc(ident_set, 1)
            pool.memset(zeros, 0.0).then_inc(zeros_set, 1)

            def probe(s, b, before):
                at_least(pool, probed, GROUP * (s - 1))
                pool.wait_ge(piece_ready, s + 1)
                pool.sem_inc(pool_past, 1)
                for i in range(GROUP):
                    gather(probe_rows[b][:, i, :], dst, piece_i[:, b, i:i + 1]).then_inc(probe_in[b], 16)

            pairwise(pool, NG, probe)
            def place_seeds():
                pool.wait_ge(edges_in, 16)
                pool.wait_ge(tgt_out, 16)
                gather(run_seed[:, :], tgt_table, re_i[:, 0:1]).then_inc(run_seed_in, 16)
                pool.wait_ge(seeds_zeroed, 16 * ZERO_PARTS)

                def scatter_seeds(g, b, before):
                    pool.wait_ge(staged, 2 * g + 2)
                    pool.sem_inc(pool_past, 1)
                    for i in range(GROUP):
                        scatter(seeds, seed_idx[:, b, i:i + 1], seed_val[:, b, i, :]).then_inc(seed_out[b], 16)

                pairwise(pool, NG, scatter_seeds)
                pool.wait_ge(first_out, 16)
                pool.wait_ge(tail_ready, 1)
                gather(tail_end_i[:, :], first_edge, tail_next_i[:, :]).then_inc(tail_end_in, 16)

            for b in range(2):
                pool.wait_ge(table_out[b], 16 * NG // 2)

            def gather_chunk(t, b, before):
                pool.wait_ge(src_in[b], 16 * (before + 1))
                pool.sem_inc(pool_past, 1)
                for c in range(CHUNK):
                    gather(rows[:, b, c, :], table, src_c[:, b, c:c + 1]).then_inc(rows_in[b], 16)

            def gather_and_seed(t, b, before):
                gather_chunk(t, b, before)
                if isinstance(t, int) and t == 0:
                    place_seeds()

            pairwise(pool, T, gather_and_seed)

            pool.wait_ge(dumped[0], 16 * ((T + 1) // 2))
            pool.wait_ge(dumped[1], 16 * (T // 2))
            pool.wait_ge(tail_step, 3)
            gather(tail_row[:, :], running[0:E, :], tail_last_i[:, :]).then_inc(tail_row_in, 16)
            pool.wait_ge(merged_ready, 1)
            scatter(running, tail_put_i[:, :], merged[:, :]).then_inc(merged_out, 16)
            pool.wait_ge(merged_out, 16)

            def gather_last(g, b, before):
                pool.wait_ge(last_staged, g + 1)
                at_least(pool, y_ready, g - 1)
                pool.sem_inc(pool_past, 1)
                for i in range(OUT_GROUP):
                    gather(fin_rows[:, b, i, :], running[0:E, :], last_idx[:, b, i:i + 1]).then_inc(fin_in[b], 16)

            pairwise(pool, NO, gather_last)

        @block.tensor
        def _(pe):
            pe.wait_ge(weights_in, 16 * 5)
            pe.wait_ge(spread_a, H)
            pe.matmul(banks[:, 7, 0:2 * H], wn[:, :], ab[:, 0:2, :].rearrange("p j h -> p (j h)"), start=True, stop=True).then_inc(vectors, 1)
            pe.matmul(banks[:, 7, 2 * H:3 * H], we2[:, :, :].rearrange("p a f -> p (a f)"), ab[:, 2, :], start=True, stop=True).then_inc(vectors, 1)
            pe.wait_ge(tail_diag, 1)
            pe.wait_ge(ones_set, 1)
            pe.matmul(banks[:, 6, 0:P], ones[:, :], diag[:, 0, :], start=True, stop=True).then_inc(tail_spread, 1)

            pe.wait_ge(ident_set, 1)
            pe.wait_ge(weights_ready, 3)
            pe.wait_ge(same_ready, 1)

            def sum_pieces(g, b, before):
                pe.wait_ge(compared, g + 1)
                at_least(pe, piece_ready, g)
                for i in range(GROUP):
                    for q in range(QT):
                        last = pe.matmul(banks[:, 7, i:i + 1], past[:, q, i, :], ones_b[:, :], start=(q == 0), stop=(q == QT - 1))
                last.then_inc(pieces_summed, 1)

            def project(g, b, before):
                pe.wait_ge(x_normed, g + 1)
                at_least(pe, ht_ready, 2 * g)
                for i in range(GROUP):
                    last = pe.transpose(banks[:, 2 * b + i // 4, (i % 4) * P:(i % 4 + 1) * P], xn[:, b, i, :], ident[:, :])
                last.then_inc(transposed[b], 1)
                pe.wait_ge(ht_ready, 2 * g + 2)
                at_least(pe, tab_ready, g)
                for i in range(GROUP):
                    last = pe.matmul(banks[:, 4 + i // 3, (i % 3) * RW:(i % 3 + 1) * RW], ht[:, i * P:(i + 1) * P], wc[:, :],
                                     start=True, stop=True)
                last.then_inc(projected, 1)

            pairwise(pe, NG, sum_pieces, project)
            pe.wait_ge(tab_ready, NG)

            def score_chunk(t, b, before):
                pe.wait_ge(feat_in[b], 16 * (before + 1))
                for i in range(PAIRS):
                    last = pe.matmul(banks[:, b, i * 2 * H:(i + 1) * 2 * H], feat_c[:, b, i, :],
                                     wscore[:, :, :].rearrange("p a h -> p (a h)"), start=True, stop=True)
                last.then_inc(scores_ready, 1)

            pairwise(pe, T, score_chunk)

            pe.wait_ge(gmax_diag, 1)
            pe.matmul(banks[:, 2, :], ones[:, :], diag[:, :, :].rearrange("p h q -> p (h q)"), start=True, stop=True).then_inc(gmax_spread, 1)
            pe.wait_ge(tail_scaled, 1)
            pe.matmul(banks[:, 3, 0:W], same[:, :], tail_s[:, :, :].rearrange("p h w -> p (h w)"), start=True, stop=True).then_inc(tail_sums, 1)

        @block.scalar
        def _(act):
            def count_piece(s, b, before):
                act.wait_ge(probe_in[b], 16 * GROUP * (before + 1))
                for i in range(GROUP):
                    at_least(act, probed, s * GROUP + i - 1)
                    act.activation(signs[:, (b + i) % 2, :], probe_rows[b][:, i, :], ACT.Sign, bias=half_id[:, bass.ds(s * GROUP + i, 1)], scale=-1.0,
                                   accum_out=below[:, bass.ds(s * GROUP + i, 1)]).then_inc(probed, 1)

            def deviation(g, b, before):
                act.wait_ge(x_var, g + 1)
                at_least(act, x_rstd, g - 1)
                act.activation(dev[:, b, :], var[:, :], ACT.Sqrt).then_inc(x_dev, 1)

            def relu(g, b, before):
                act.wait_ge(transposed[b], before + 1)
                at_least(act, projected, g)
                flat = banks[:, 2 * b:2 * b + 2, :].rearrange("p a n -> p (a n)")
                act.activation(ht[:, 0:4 * P], flat[:, 0:4 * P], ACT.Relu).then_inc(ht_ready, 1)
                act.activation(ht[:, 4 * P:GROUP * P], flat[:, 4 * P:GROUP * P], ACT.Relu).then_inc(ht_ready, 1)

            def take_rows(g, b, before):
                act.wait_ge(projected, g + 1)
                at_least(act, table_out[b], 16 * before)
                act.activation(tab[:, b, 0:GROUP - 1, :].rearrange("p (a i) w -> p a (i w)", i=3), banks[:, 4:6, 0:3 * RW], ACT.Copy)
                act.activation(tab[:, b, GROUP - 1, :], banks[:, 6, 0:RW], ACT.Copy).then_inc(tab_ready, 1)
                act.wait_ge(tab_ready, g + 1)
                act.activation(tgt_all[:, bass.ds(g * GROUP, GROUP), :], tab[:, b, :, W:RW], ACT.Copy).then_inc(tgt_kept, 1)
                act.dma_start(table_v[:, bass.ds(g * GROUP, GROUP), :], tab[:, b, :, 0:W]).then_inc(table_out[b], 16)

            def relu_and_count(g, b, before):
                relu(g, b, before)
                count_piece(g, b, before)
                take_rows(g, b, before)

            pairwise(act, NG, deviation, relu_and_count)

            act.wait_ge(nodes_placed, 3)
            act.wait_ge(tgt_kept, NG)

            def stage_seeds(g, b, before):
                at_least(act, seed_out[b], 16 * GROUP * before)
                act.activation(seed_idx[:, b, :], seed_at[:, bass.ds(g * GROUP, GROUP)], ACT.Copy).then_inc(staged, 1)
                act.activation(seed_val[:, b, :, :], tgt_all[:, bass.ds(g * GROUP, GROUP), :], ACT.Copy).then_inc(staged, 1)

            pairwise(act, NG, stage_seeds)

            def exps(t, b):
                act.wait_ge(expo_ready, t + 1)
                act.activation(expd[:, :, :, :], expo[:, :, :, :], ACT.Exp).then_inc(exps_ready, 1)

            def widen(t, b):
                act.wait_ge(fade_ready, t + 1)
                at_least(act, summed, t - 1)
                act.activation(fade_w[:, b, :, :, :], fade[:, b, :, None, :].to_broadcast([P, H, HW, SLOTS]), ACT.Copy).then_inc(fade_wide, 1)

            def carry(t, b):
                act.wait_ge(summed, t)
                act.activation(terms[:, :, :, 0], sums[:, 1 - b, :, :, CHUNK], ACT.Copy).then_inc(carried, 1)

            def empty(t, b, before):
                act.wait_ge(summed, t + 1)
                at_least(act, dumped[b], 16 * before)
                act.activation(dump[:, b, :, 0:W].rearrange("p c (h w) -> p h w c", h=H), sums[:, b, :, :, 1:SLOTS], ACT.Copy)
                act.activation(dump[:, b, :, W:RW].rearrange("p c h -> p h c"), top[:, b, :, 1:SLOTS], ACT.Copy).then_inc(dump_ready, 1)

            def weights(t, b, before):
                exps(t, b)
                widen(t, b)
                if not (isinstance(t, int) and t == 0):
                    carry(t, b)

            pairwise(act, T, weights, empty)

            act.wait_ge(tail_max, 1)
            act.activation(ge[:, :, :], gd[:, :, :], ACT.Exp).then_inc(tail_scale, 1)

            def stage_last(g, b, before):
                at_least(act, fin_in[b], 16 * OUT_GROUP * before)
                act.activation(last_idx[:, b, :], last_at[:, bass.ds(g * OUT_GROUP, OUT_GROUP)], ACT.Copy).then_inc(last_staged, 1)

            def fin_exps(g, b, before):
                act.wait_ge(fin_exp_in, g + 1)
                act.activation(d1[:, :, :], fin_top[:, :, :], ACT.Exp, scale=-1.0).then_inc(fin_exp, 1)

            pairwise(act, NO, stage_last, fin_exps)

        @block.vector
        def _(dve):
            dve.wait_ge(heads_in, 16)
            dve.tensor_copy(head[:, 0, :], heads_i[:, :]).then_inc(ids_ready, 1)
            dve.memset(ones_b[:, :], 1.0)
            dve.wait_ge(node_iota, 3)
            dve.tensor_copy(group_id[:, :, :], group_i[:, :, :])
            dve.tensor_copy(run_spare[:, :], run_spare_i[:, :])
            dve.tensor_copy(node_id[:, :], node_i[:, :]).then_inc(ids_ready, 1)
            dve.tensor_scalar(half_id[:, :], node_i[:, 0:KT], -0.5, None, ALU.add)
            dve.memset(ab[:, :, :], 0.0).then_inc(cleared, 1)
            dve.memset(wscore[:, :, :], 0.0).then_inc(cleared, 1)
            dve.wait_ge(ids_ready, 2)

            def compare(s, b, before):
                at_least(dve, heads_moved, s)
                at_least(dve, pieces_summed, s)
                for q in range(QT):
                    last = dve.tensor_scalar(past[:, q, :, :], group_id[:, :, :], head[:, b, q:q + 1], None, ALU.is_gt)
                last.then_inc(compared, 1)
                dve.tensor_scalar(head[:, 1 - b, :], head[:, b, :], -float(GROUP), None, ALU.add).then_inc(heads_moved, 1)

            def find_piece(s, b, before):
                dve.wait_ge(pieces_summed, s + 1)
                at = bass.ds(s * GROUP, GROUP)
                dve.tensor_scalar(piece[:, at], banks[:, 7, 0:GROUP], -1.0, 0.0, ALU.add, ALU.max)
                at_least(dve, probe_in[b], 16 * GROUP * before)
                dve.tensor_scalar(piece_i[:, b, :], banks[:, 7, 0:GROUP], -1.0, 0.0, ALU.add, ALU.max).then_inc(piece_ready, 1)

            dve.wait_ge(cleared, 2)
            dve.wait_ge(weights_in, 16 * 5)
            for h in range(H):
                dve.tensor_copy(ab[HD * h:HD * (h + 1), :, h], ac[HD * h:HD * (h + 1), :]).then_inc(spread_a, 1)
            dve.wait_ge(vectors, 2)
            dve.tensor_copy(wc[:, 0:W].rearrange("p (h w) -> p h w", h=H)[:, :, HD], banks[:, 7, 0:H])
            dve.tensor_copy(wc[:, W:RW], banks[:, 7, H:2 * H]).then_inc(weights_ready, 1)
            for half in range(2):
                dve.tensor_copy(wscore[FE * half:FE * (half + 1), half, :], banks[FE * half:FE * (half + 1), 7, 2 * H:3 * H]).then_inc(weights_ready, 1)

            step = 0

            def link(s, ins):
                nonlocal step
                step += 1
                ins.then_inc(s, 1)
                dve.wait_ge(s, step)

            dve.wait_ge(edges_in, 16)
            link(edge_step, dve.tensor_copy(re[:, :], re_i[:, :]))
            link(edge_step, dve.tensor_tensor(cont[:, :], re[:, 1:2], re[:, 2:3], ALU.is_equal))
            link(edge_step, dve.scalar_tensor_tensor(tail_id[:, :], re[:, 1:2], 1.0, cont[:, :], ALU.add, ALU.mult))
            link(edge_step, dve.tensor_scalar(tail_id[:, :], tail_id[:, :], -1.0, None, ALU.add))
            link(edge_step, dve.tensor_tensor(bt[:, 0:1], re[:, 3:4], re[:, 1:2], ALU.is_equal))
            link(edge_step, dve.tensor_tensor(bt[:, 1:2], re[:, 3:4], re[:, 4:5], ALU.is_equal))
            link(edge_step, dve.tensor_tensor(bt[:, 2:3], bt[:, 0:1], bt[:, 1:2], ALU.mult))
            link(edge_step, dve.tensor_scalar(bt[:, 3:4], bt[:, 2:3], -1.0, 1.0, ALU.mult, ALU.add))
            link(edge_step, dve.tensor_tensor(rep[:, :], bt[:, 3:4], cont[:, :], ALU.mult))
            dve.tensor_scalar(tail_next_i[:, :], re[:, 1:2], 1.0, None, ALU.add).then_inc(tail_ready, 1)
            dve.wait_ge(ident_set, 1)
            dve.tensor_scalar(diag[:, 0, :], ident[:, :], tail_id[:, 0:1], None, ALU.mult).then_inc(tail_diag, 1)
            dve.wait_ge(tail_spread, 1)
            dve.tensor_scalar(same[:, :], banks[:, 6, 0:P], tail_id[:, 0:1], None, ALU.is_equal).then_inc(same_ready, 1)

            def moments(g, b, before):
                for n, (i, j) in enumerate(X_PARTS):
                    if isinstance(g, int) and i == g // 2 or not isinstance(g, int) and i > 0:
                        dve.wait_ge(x_part[n][b], 16)
                at_least(dve, x_normed, g - 1)
                for i in range(GROUP):
                    last = dve.bn_stats(st[:, i, :], x_all[b][:, bass.ds(before * (GROUP * D) + i * D, D)])
                last.then_inc(x_stats, 1)
                dve.wait_ge(x_stats, g + 1)
                dve.sem_inc(dve_past, 1)
                for i in range(GROUP):
                    last = dve.bn_aggr(mv[:, b, i, :], st[:, i, :])
                last.then_inc(x_aggr, 1)
                at_least(dve, x_dev, g)
                dve.wait_ge(x_aggr, g + 1)
                dve.tensor_scalar(var[:, :], mv[:, b, :, 1], EPS, None, ALU.add).then_inc(x_var, 1)

            def normalize(g, b, before):
                dve.wait_ge(x_dev, g + 1)
                at_least(dve, x_normed, g)
                dve.reciprocal(rstd[:, :], dev[:, b, :]).then_inc(x_rstd, 1)
                dve.wait_ge(x_rstd, g + 1)
                at_least(dve, transposed[b], before)
                for i in range(GROUP):
                    last = dve.tensor_scalar(xn[:, b, i, :], x_all[b][:, bass.ds(before * (GROUP * D) + i * D, D)], mv[:, b, i, 0:1], rstd[:, i:i + 1], ALU.subtract, ALU.mult)
                last.then_inc(x_normed, 1)

            def find_and_measure(t, b, before):
                compare(t, b, before)
                moments(t, b, before)
                if not (isinstance(t, int) and t == 0):
                    normalize(t - 1, 1 - b, before if b else before - 1)
                find_piece(t, b, before)

            pairwise(dve, NG, find_and_measure)
            normalize(NG - 1, 1, NG // 2 - 1)

            step = 0
            link(node_step, dve.memset(fe[:, KT:KT + 1], float(E)))
            dve.wait_ge(probed, KT)
            link(node_step, dve.tensor_scalar(below[:, :], below[:, :], 0.5, HEAD / 2, ALU.mult, ALU.add))
            dve.scalar_tensor_tensor(fe[:, 0:KT], piece[:, :], float(HEAD), below[:, :], ALU.mult, ALU.add).then_inc(located, 1)
            dve.wait_ge(shifted, 16)
            link(node_step, dve.tensor_tensor(deg[:, :], fe[:, 1:KT + 1], fe[:, 0:KT], ALU.subtract))
            link(node_step, dve.tensor_scalar(some[:, :], deg[:, :], 0.0, None, ALU.is_gt))
            link(node_step, dve.tensor_scalar(none_n[:, :], deg[:, :], -1.0, float(E), ALU.mult, ALU.add))
            link(node_step, dve.tensor_scalar(spare[:, :], node_id[:, 0:KT], float(E), None, ALU.add))
            link(node_step, dve.tensor_tensor(seed_at[:, :], fe[:, 0:KT], spare[:, :], ALU.subtract))
            link(node_step, dve.tensor_tensor(seed_at[:, :], seed_at[:, :], some[:, :], ALU.mult))
            dve.tensor_copy(fe_i[:, :], fe[:, 0:KT]).then_inc(nodes_placed, 1)
            dve.tensor_tensor(seed_at[:, :], seed_at[:, :], spare[:, :], ALU.add).then_inc(nodes_placed, 1)
            dve.tensor_scalar(last_at[:, :], fe[:, 1:KT + 1], -1.0, 0.0, ALU.add, ALU.max).then_inc(nodes_placed, 1)

            dve.memset(keep[:, :, 0], 0.0)
            for b in range(2):
                dve.memset(fade[:, b, :, 0], 0.0)
                dve.memset(top[:, b, :, :], 0.0)
            dve.memset(tgt_s[:, :, CHUNK], 0.0)
            dve.wait_ge(seeds_zeroed, 16 * ZERO_PARTS)
            dve.memset(terms[:, :, :, 0], 0.0).then_inc(carries, 1)
            dve.wait_ge(carries, 1)

            def scan(dst_ap, factors, plus, combine):
                return dve.tensor_tensor_scan(dst_ap, factors, plus, 0.0, ALU.mult, combine)

            def flat(ap):
                return ap.rearrange("p h s -> p (h s)")

            def flat4(ap):
                return ap.rearrange("p h w s -> p (h w s)")

            def chunk(t, b, before):
                at_least(dve, summed, t)
                dve.wait_ge(dstc_in[b], 16 * (before + 1))
                dve.tensor_tensor(keep[:, :, 1:SLOTS], dst_c[:, b, None, 1:SLOTS].to_broadcast([P, H, CHUNK]),
                                  dst_c[:, b, None, 0:CHUNK].to_broadcast([P, H, CHUNK]), ALU.is_equal).then_inc(kept, 1)
                dve.wait_ge(seed_in[b], 16 * (before + 1))
                dve.tensor_copy(seed_s[:, :, 0], tgt_s[:, :, CHUNK])
                dve.tensor_copy(seed_s[:, :, 1:SLOTS], seed_c[:, b, :, :].rearrange("p c h -> p h c")).then_inc(seeded, 1)
                dve.wait_ge(seeded, t + 1)
                dve.wait_ge(kept, t + 1)
                scan(flat(tgt_s[:, :, :]), flat(keep[:, :, :]), flat(seed_s[:, :, :]), ALU.add).then_inc(tgt_filled, 1)
                dve.wait_ge(tgt_filled, t + 1)
                dve.wait_ge(scores_ready, t + 1)
                dve.tensor_tensor(att[:, :, :], banks[:, b, 0:CHUNK * H].rearrange("p (c h) -> p h c", h=H), tgt_s[:, :, 1:SLOTS], ALU.add).then_inc(added, 1)
                dve.wait_ge(added, t + 1)
                dve.wait_ge(rows_in[b], 16 * CHUNK * (before + 1))
                rows_h = rows[:, b, :, :].rearrange("p c (h w) -> p h w c", h=H)
                dve.tensor_tensor(att[:, :, :], att[:, :, :], rows_h[:, :, HD, :], ALU.add).then_inc(scored, 1)
                dve.wait_ge(scored, t + 1)
                dve.scalar_tensor_tensor(att[:, :, :], att[:, :, :], SLOPE, att[:, :, :], ALU.mult, ALU.max).then_inc(leaked, 1)
                dve.wait_ge(leaked, t + 1)
                dve.tensor_copy(att_s[:, :, 0], top[:, 1 - b, :, CHUNK])
                dve.tensor_scalar(att_s[:, :, 1:SLOTS], att[:, :, :], 0.0, None, ALU.max).then_inc(floored, 1)
                dve.wait_ge(floored, t + 1)
                at_least(dve, dump_ready, t - 1)
                scan(flat(top[:, b, :, :]), flat(keep[:, :, :]), flat(att_s[:, :, :]), ALU.max).then_inc(topped, 1)
                dve.wait_ge(topped, t + 1)
                dve.tensor_tensor(expo[:, 0, :, :], keep[:, :, 1:SLOTS], top[:, b, :, 0:CHUNK], ALU.mult).then_inc(faded, 1)
                dve.tensor_tensor(expo[:, 1, :, :], att[:, :, :], top[:, b, :, 1:SLOTS], ALU.subtract)
                dve.wait_ge(faded, t + 1)
                dve.tensor_tensor(expo[:, 0, :, :], expo[:, 0, :, :], top[:, b, :, 1:SLOTS], ALU.subtract).then_inc(expo_ready, 1)
                dve.memset(rows_h[:, :, HD, :], 1.0)
                dve.wait_ge(exps_ready, t + 1)
                dve.scalar_tensor_tensor(expd[:, 0, :, :], expo[:, 0, :, :], 0.0, expd[:, 0, :, :], ALU.is_ge, ALU.max).then_inc(held, 1)
                dve.wait_ge(held, t + 1)
                dve.scalar_tensor_tensor(fade[:, b, :, 1:SLOTS], expd[:, 0, :, :], 1.0, keep[:, :, 1:SLOTS], ALU.min, ALU.mult).then_inc(fade_ready, 1)
                at_least(dve, summed, t)
                dve.wait_ge(fade_ready, t + 1)
                dve.tensor_tensor(terms[:, :, :, 1:SLOTS], rows_h, expd[:, 1, :, None, :].to_broadcast([P, H, HW, CHUNK]), ALU.mult).then_inc(terms_ready, 1)
                dve.wait_ge(terms_ready, t + 1)
                dve.wait_ge(fade_wide, t + 1)
                at_least(dve, carried, t)
                at_least(dve, dump_ready, t - 1)
                scan(flat4(sums[:, b, :, :, :]), flat4(fade_w[:, b, :, :, :]), flat4(terms[:, :, :, :]), ALU.add).then_inc(summed, 1)

            pairwise(dve, T, chunk)

            dve.wait_ge(tail_end_in, 16)
            step = 0
            dve.tensor_scalar(tail_last_i[:, :], tail_end_i[:, :], -1.0, None, ALU.add)
            link(tail_step, dve.tensor_scalar(tail_end[:, :], tail_end_i[:, :], -1.0, None, ALU.add))
            link(tail_step, dve.scalar_tensor_tensor(tail_put[:, :], tail_end[:, :], run_spare[:, 0:1], rep[:, :], ALU.subtract, ALU.mult))
            link(tail_step, dve.tensor_tensor(tail_put_i[:, :], tail_put[:, :], run_spare[:, :], ALU.add))

            dve.wait_ge(topped, T)
            dve.tensor_tensor(diag[:, :, :], ident[:, None, :].to_broadcast([P, H, P]), top[:, 0, :, CHUNK:SLOTS].to_broadcast([P, H, P]), ALU.mult).then_inc(gmax_diag, 1)
            dve.wait_ge(gmax_spread, 1)
            link(tail_step, dve.tensor_tensor(mask4[:, :, :], banks[:, 2, :].rearrange("p (h q) -> p h q", h=H), same[:, None, :].to_broadcast([P, H, P]), ALU.mult))
            link(tail_step, dve.tensor_reduce(gmax[:, :], mask4[:, :, :], AX_X, ALU.max))
            dve.wait_ge(tail_row_in, 16)
            link(tail_step, dve.tensor_tensor(merged[:, W:RW], gmax[:, :], tail_row[:, W:RW], ALU.max))
            dve.tensor_tensor(gd[:, 0, :], top[:, 0, :, CHUNK], merged[:, W:RW], ALU.subtract)
            dve.tensor_tensor(gd[:, 1, :], tail_row[:, W:RW], merged[:, W:RW], ALU.subtract).then_inc(tail_max, 1)
            dve.wait_ge(tail_scale, 1)
            dve.wait_ge(summed, T)
            dve.tensor_tensor(tail_s[:, :, :], sums[:, 0, :, :, CHUNK], ge[:, 0, :, None].to_broadcast([P, H, HW]), ALU.mult).then_inc(tail_scaled, 1)
            row_h = tail_row[:, 0:W].rearrange("p (h w) -> p h w", h=H)
            link(tail_step, dve.tensor_tensor(row_h, row_h, ge[:, 1, :, None].to_broadcast([P, H, HW]), ALU.mult))
            dve.wait_ge(tail_sums, 1)
            dve.tensor_tensor(merged[:, 0:W], banks[:, 3, 0:W], tail_row[:, 0:W], ALU.add).then_inc(merged_ready, 1)

            def finish(g, b, before):
                dve.wait_ge(fin_in[b], 16 * OUT_GROUP * (before + 1))
                fin_h = fin_rows[:, b, :, 0:W].rearrange("p k (h w) -> p k h w", h=H)
                at = bass.ds(g * OUT_GROUP, OUT_GROUP)
                dve.tensor_copy(fin_top[:, :, :], fin_rows[:, b, :, W:RW]).then_inc(fin_exp_in, 1)
                dve.wait_ge(fin_exp, g + 1)
                dve.tensor_tensor(d2[:, :, :], d1[:, :, :], none_n[:, at, None].to_broadcast([P, OUT_GROUP, H]), ALU.mult).then_inc(fin_step, 1)
                dve.wait_ge(fin_step, 4 * g + 1)
                dve.tensor_tensor(d2[:, :, :], d2[:, :, :], fin_h[:, :, :, HD], ALU.add).then_inc(fin_step, 1)
                dve.wait_ge(fin_step, 4 * g + 2)
                dve.reciprocal(d2[:, :, :], d2[:, :, :]).then_inc(fin_step, 1)
                dve.wait_ge(fin_step, 4 * g + 3)
                dve.tensor_tensor(d2[:, :, :], d2[:, :, :], some[:, at, None].to_broadcast([P, OUT_GROUP, H]), ALU.mult).then_inc(fin_step, 1)
                dve.wait_ge(fin_step, 4 * g + 4)
                at_least(dve, y_out[b], 16 * before)
                y_h = y_g[:, b, :, :].rearrange("p k (h w) -> p k h w", h=H)
                dve.tensor_tensor(y_h, fin_h[:, :, :, 0:HD], d2[:, :, :, None].to_broadcast([P, OUT_GROUP, H, HD]), ALU.mult).then_inc(fin_free, 1)
                dve.wait_ge(fin_free, g + 1)
                dve.wait_ge(xg_in[b], 16 * (before + 1))
                dve.tensor_tensor(y_g[:, b, :, :], y_g[:, b, :, :], x_g[:, b, :, :], ALU.add).then_inc(y_ready, 1)

            pairwise(dve, NO, finish)


def kernel(**inputs):
    import numpy as np
    import concourse.bacc as bacc
    from concourse.bass_utils import run_bass_kernel_spmd

    x, src, dst = (np.asarray(inputs[n]) for n in ("x", "src", "dst"))
    feats = np.asarray(inputs["edge_attr_64"])
    w_node, w_edge, a = (np.asarray(inputs[f"L0_gnn_{n}"]) for n in ("W_node", "W_edge", "a"))
    nodes, d = x.shape
    edges, fe = feats.shape
    run = edges // P
    chunks = run // CHUNK
    heads = edges // 625
    padded = -(-nodes // (2 * GROUP * P)) * (2 * GROUP * P)
    x_rows = np.zeros((padded, d), x.dtype)
    x_rows[:nodes] = x
    dst_runs = np.full((P, run + 1), -1, dst.dtype)
    dst_runs[:, 1:] = dst.reshape(P, run)
    run_edges = np.full((P + 2, 5), -1, dst.dtype)
    run_edges[:P, 0], run_edges[:P, 1] = dst_runs[:, 1], dst_runs[:, -1]
    run_edges[:P - 1, 2:4] = run_edges[1:P, 0:2]
    run_edges[:P - 2, 4] = run_edges[2:P, 0]
    cols = np.zeros((P, chunks, SLOTS, fe), feats.dtype)
    cols[:, :, :CHUNK] = feats.reshape(P, chunks, CHUNK, fe)
    feats_t = cols.reshape(P, chunks, SLOTS // 2, 2, fe).transpose(1, 3, 4, 2, 0).reshape(chunks * 2 * fe, -1)
    n_heads, hd = a.shape[0], a.shape[1] // 3
    arrays = {
        "x": x_rows,
        "src": src.reshape(P, run),
        "dst_runs": dst_runs,
        "dst": dst.reshape(heads, -1),
        "heads": dst.reshape(heads, -1)[:, 0].reshape(-1, P).T,
        "run_edges": run_edges[:P],
        "feats": feats_t,
        "w_node": w_node,
        "w_node_t": w_node.T,
        "w_edge": w_edge,
        "a_cols": a.reshape(n_heads, 3, hd).transpose(0, 2, 1).reshape(n_heads * hd, 3),
    }
    arrays = {n: np.ascontiguousarray(v) for n, v in arrays.items()}
    nc = bacc.Bacc("TRN2", target_bir_lowering=False, num_devices=1)
    args = {n: nc.dram_tensor(f"in_{n}", v.shape, mybir.dt.from_np(v.dtype), kind="ExternalInput").ap() for n, v in arrays.items()}
    out = nc.dram_tensor("out", (padded, d), F32, kind="ExternalOutput").ap()
    gnn_kernel(nc, **args, out=out)
    r = run_bass_kernel_spmd(nc, [{f"in_{n}": v for n, v in arrays.items()}], core_ids=[0])
    return r.results[0]["out"][:nodes]
```

```python
from contextlib import ExitStack

import concourse.bass as bass
from concourse import mybir

F32 = mybir.dt.float32
BF16 = mybir.dt.bfloat16
I32 = mybir.dt.int32
ALU = mybir.AluOpType
ACT = mybir.ActivationFunctionType
AX_X = mybir.AxisListType.X

P = 128

CHUNK = 25
SLOTS = CHUNK + 1
GROUP = 7
OUT_GROUP = 7
EPS = 1e-5
SLOPE = 0.2
ZERO_PARTS = 5


def gnn_kernel(nc, x, src, dst_runs, dst, heads, run_edges, feats, w_node, w_node_t, w_edge, a_cols, out):
    E, N, D = dst.shape[0] * dst.shape[1], out.shape[0], out.shape[1]
    H = 4
    HD = D // H
    FE = w_edge.shape[1]
    RUN = E // P
    T = RUN // CHUNK
    PAIRS = SLOTS // 2
    KT = N // P
    HW = HD + 1
    W = H * HW
    RW = W + H
    HEADS, HEAD = dst.shape
    QT = HEADS // P
    NG, NO = KT // GROUP, KT // OUT_GROUP
    assert HEADS == QT * P and RUN == T * CHUNK and T % 2 == 1 and N == KT * P and KT % (2 * GROUP) == 0

    table = nc.dram_tensor("table", (N, W), F32).ap()
    tgt_table = nc.dram_tensor("tgt_table", (N, H), F32).ap()
    first_edge = nc.dram_tensor("first_edge", (N, 1), I32).ap()
    seeds = nc.dram_tensor("seeds", (E + N, H), F32).ap()
    running = nc.dram_tensor("running", (E + P, RW), F32).ap()
    table_v = table.rearrange("(p k) w -> p k w", p=P)
    tgt_table_v = tgt_table.rearrange("(p k) h -> p (k h)", p=P)
    first_edge_v = first_edge.rearrange("(p k) o -> p (k o)", p=P)
    seeds_v = seeds[0:E, :].rearrange("(p c) h -> p (c h)", p=P)
    running_v = running[0:E, :].rearrange("(p c) w -> p (c w)", p=P)
    x_v = x.rearrange("(p k) d -> p (k d)", p=P)
    out_v = out.rearrange("(p k) d -> p (k d)", p=P)

    with ExitStack() as ctx:
        def sb(name, shape, dt=F32):
            return ctx.enter_context(nc.sbuf_tensor(name, shape, dt))

        def sem(name):
            return ctx.enter_context(nc.semaphore(name))

        wn = sb("wn", [P, D])
        we2 = sb("we2", [P, 2, FE])
        ac = sb("ac", [P, 3])
        ab = sb("ab", [P, 3, H])
        wc = sb("wc", [P, RW])
        wscore = sb("wscore", [P, 2, H])
        ident = sb("ident", [P, P])
        ones = sb("ones", [P, P])
        node_i = sb("node_i", [P, KT + 1], I32)
        node_id = sb("node_id", [P, KT + 1])
        group_i = sb("group_i", [P, GROUP, P], I32)
        group_id = sb("group_id", [P, GROUP, P])
        heads_i = sb("heads_i", [P, QT], I32)
        head = sb("head", [P, 2, QT])
        past = sb("past", [P, QT, GROUP, P], BF16)
        ones_b = sb("ones_b", [P, 1], BF16)
        signs = sb("signs", [P, 2, HEAD])
        piece = sb("piece", [P, KT])
        piece_i = sb("piece_i", [P, 2, GROUP], I32)
        below = sb("below", [P, KT])
        half_id = sb("half_id", [P, KT])
        fe = sb("fe", [P, KT + 1])
        fe_i = sb("fe_i", [P, KT], I32)
        deg = sb("deg", [P, KT])
        some = sb("some", [P, KT])
        none_n = sb("none_n", [P, KT])
        spare = sb("spare", [P, KT])
        seed_at = sb("seed_at", [P, KT])
        last_at = sb("last_at", [P, KT])
        tgt_all = sb("tgt_all", [P, KT, H])
        seed_idx = sb("seed_idx", [P, 2, GROUP], I32)
        seed_val = sb("seed_val", [P, 2, GROUP, H])
        last_idx = sb("last_idx", [P, 2, OUT_GROUP], I32)
        xn = sb("xn", [P, 2, GROUP, D])
        st = sb("st", [P, GROUP, 6])
        mv = sb("mv", [P, 2, GROUP, 2])
        var = sb("var", [P, GROUP])
        dev = sb("dev", [P, 2, GROUP])
        rstd = sb("rstd", [P, GROUP])
        ht = sb("ht", [P, GROUP * D])
        tab = sb("tab", [P, 2, GROUP, RW])
        re_i = sb("re_i", [P, 5], I32)
        re = sb("re", [P, 5])
        cont = sb("cont", [P, 1])
        tail_id = sb("tail_id", [P, 1])
        bt = sb("bt", [P, 4])
        rep = sb("rep", [P, 1])
        diag = sb("diag", [P, H, P])
        same = sb("same", [P, P])
        tail_next_i = sb("tail_next_i", [P, 1], I32)
        tail_end_i = sb("tail_end_i", [P, 1], I32)
        tail_end = sb("tail_end", [P, 1])
        tail_last_i = sb("tail_last_i", [P, 1], I32)
        tail_put = sb("tail_put", [P, 1])
        tail_put_i = sb("tail_put_i", [P, 1], I32)
        run_seed = sb("run_seed", [P, H])
        src_c = sb("src_c", [P, 2, CHUNK], I32)
        dst_c = sb("dst_c", [P, 2, SLOTS], I32)
        seed_c = sb("seed_c", [P, 2, CHUNK, H])
        feat_c = sb("feat_c", [P, 2, PAIRS, P])
        rows = sb("rows", [P, 2, CHUNK, W])
        keep = sb("keep", [P, H, SLOTS])
        seed_s = sb("seed_s", [P, H, SLOTS])
        tgt_s = sb("tgt_s", [P, H, SLOTS])
        att = sb("att", [P, H, CHUNK])
        att_s = sb("att_s", [P, H, SLOTS])
        top = sb("top", [P, 2, H, SLOTS])
        expo = sb("expo", [P, 2, H, CHUNK])
        expd = sb("expd", [P, 2, H, CHUNK])
        fade = sb("fade", [P, 2, H, SLOTS])
        fade_w = sb("fade_w", [P, 2, H, HW, SLOTS])
        terms = sb("terms", [P, H, HW, SLOTS])
        sums = sb("sums", [P, 2, H, HW, SLOTS])
        dump = sb("dump", [P, 2, CHUNK, RW])

        def flat_part(buffer, dims, n):
            return buffer.rearrange(f"p {dims} -> p ({dims})")[:, 0:n]

        probe_rows = [r.rearrange("p (i e) -> p i e", e=HEAD).bitcast(I32) for r in
                      (flat_part(dump[:, :, :, :], "b c w", GROUP * HEAD), flat_part(sums[:, :, :, :, :], "b h w s", GROUP * HEAD))]
        zeros = flat_part(terms[:, :, :, :], "h w s", RUN * H // ZERO_PARTS)
        x_all = [flat_part(rows[:, :, :, :], "b c w", KT * D // 2), flat_part(fade_w[:, :, :, :, :], "b h w s", KT * D // 2)]
        def as_groups(buffer, dims, width):
            return flat_part(buffer, dims, 2 * OUT_GROUP * width).rearrange("p (b k w) -> p b k w", b=2, k=OUT_GROUP)

        fin_rows = as_groups(dump[:, :, :, :], "b c w", RW)
        x_g = as_groups(rows[:, :, :, :], "b c w", D)
        y_g = as_groups(fade_w[:, :, :, :, :], "b h w s", D)
        d1 = sb("d1", [P, OUT_GROUP, H])
        d2 = sb("d2", [P, OUT_GROUP, H])
        fin_top = sb("fin_top", [P, OUT_GROUP, H])
        run_spare_i = sb("run_spare_i", [P, 1], I32)
        run_spare = sb("run_spare", [P, 1])
        gmax = sb("gmax", [P, H])
        gd = sb("gd", [P, 2, H])
        ge = sb("ge", [P, 2, H])
        mask4 = sb("mask4", [P, H, P])
        tail_row = sb("tail_row", [P, RW])
        tail_s = sb("tail_s", [P, H, HW])
        merged = sb("merged", [P, RW])

        banks = ctx.enter_context(nc.psum_tensor("banks", [P, 8, 512], F32))

        def pair(name):
            return [sem(f"{name}{b}") for b in range(2)]

        heads_in, weights_in, edges_in = sem("heads_in"), sem("weights_in"), sem("edges_in")
        zeros_set, seeds_zeroed = sem("zeros_set"), sem("seeds_zeroed")
        node_iota, ident_zero, ident_set, ones_set, ids_ready = (
            sem("node_iota"), sem("ident_zero"), sem("ident_set"), sem("ones_set"), sem("ids_ready"))
        cleared, spread_a, vectors, weights_ready = sem("cleared"), sem("spread_a"), sem("vectors"), sem("weights_ready")
        x_first, x_next = pair("x_first"), pair("x_next")
        shifted, held, halved = sem("shifted"), sem("held"), sem("halved")
        located, pool_past, dve_past = sem("located"), sem("pool_past"), sem("dve_past")
        heads_moved, compared, pieces_summed, piece_ready, probe_in, probed = (
            sem("heads_moved"), sem("compared"), sem("pieces_summed"), sem("piece_ready"), pair("probe_in"), sem("probed"))
        x_stats, x_aggr, x_var, x_dev, x_rstd, x_normed = sem("x_stats"), sem("x_aggr"), sem("x_var"), sem("x_dev"), sem("x_rstd"), sem("x_normed")
        transposed, ht_ready, projected, tab_ready, table_out, tgt_kept = (
            pair("transposed"), sem("ht_ready"), sem("projected"), sem("tab_ready"), pair("table_out"), sem("tgt_kept"))
        tgt_out, node_step, nodes_placed, first_out = sem("tgt_out"), sem("node_step"), sem("nodes_placed"), sem("first_out")
        edge_step, tail_diag, tail_spread, same_ready, tail_ready, tail_end_in, tail_step = (
            sem("edge_step"), sem("tail_diag"), sem("tail_spread"), sem("same_ready"), sem("tail_ready"), sem("tail_end_in"), sem("tail_step"))
        run_seed_in, staged, seed_out, seeds_ready = sem("run_seed_in"), sem("staged"), pair("seed_out"), sem("seeds_ready")
        src_in, dstc_in, seed_in, feat_in, rows_in = pair("src_in"), pair("dstc_in"), pair("seed_in"), pair("feat_in"), pair("rows_in")
        carries, scores_ready, kept, seeded, tgt_filled, added, scored, leaked, floored, topped = (
            sem("carries"), sem("scores_ready"), sem("kept"), sem("seeded"), sem("tgt_filled"), sem("added"), sem("scored"), sem("leaked"),
            sem("floored"), sem("topped"))
        faded, expo_ready, exps_ready, fade_ready, fade_wide, carried, terms_ready, summed = (
            sem("faded"), sem("expo_ready"), sem("exps_ready"), sem("fade_ready"), sem("fade_wide"), sem("carried"), sem("terms_ready"),
            sem("summed"))
        dump_ready, dumped = sem("dump_ready"), pair("dumped")
        gmax_diag, gmax_spread, tail_max, tail_scale, tail_scaled, tail_sums, tail_row_in, merged_ready, merged_out = (
            sem("gmax_diag"), sem("gmax_spread"), sem("tail_max"), sem("tail_scale"), sem("tail_scaled"), sem("tail_sums"),
            sem("tail_row_in"), sem("merged_ready"), sem("merged_out"))
        last_staged, fin_in, xg_in, fin_step, fin_exp_in, fin_exp, fin_free, y_ready, y_out = (
            sem("last_staged"), pair("fin_in"), pair("xg_in"), sem("fin_step"), sem("fin_exp_in"), sem("fin_exp"), sem("fin_free"),
            sem("y_ready"), pair("y_out"))

        block = ctx.enter_context(nc.Block())

        def at_least(eng, s, value):
            if not (isinstance(value, int) and value <= 0):
                eng.wait_ge(s, value)

        def pairwise(eng, n, step, lagging=None, lag=1, more=0, after=0):
            def both(t, b, before):
                step(t, b, before)
                if lagging and not (isinstance(t, int) and t < lag):
                    if lag == 1:
                        lagging(t - 1, 1 - b, before if b else before - 1)
                    else:
                        lagging(t - 2, b, before - 1)

            peeled = 2 + n % 2 + more
            for t in range(peeled):
                both(t, t % 2, t // 2)
            with eng.Fori(0, (n - after - peeled) // 2) as j:
                for i in range(2):
                    both(peeled + 2 * j + i, (peeled + i) % 2, (peeled + i) // 2 + j)
            for t in range(n - after, n):
                both(t, t % 2, t // 2)
            if lagging:
                for t in range(n - lag, n):
                    lagging(t, t % 2, t // 2)

        assert NG % 2 == 0


        @block.sync
        def _(sp):
            sp.dma_start(heads_i[:, :], heads).then_inc(heads_in, 16)
            sp.dma_start(wn[:, :], w_node).then_inc(weights_in, 16)
            sp.dma_start(wc[:, 0:W].rearrange("p (h w) -> p h w", h=H)[:, :, 0:HD],
                         w_node_t.rearrange("p (h w) -> p h w", h=H)).then_inc(weights_in, 16)
            for half in range(2):
                sp.dma_start(we2[:, half, :], w_edge).then_inc(weights_in, 16)
            sp.dma_start(ac[:, :], a_cols).then_inc(weights_in, 16)
            sp.dma_start(re_i[:, :], run_edges).then_inc(edges_in, 16)
            x_pairs = x_v.rearrange("p (a b n) -> p b a n", b=2, n=GROUP * D)
            x_to = [x_all[b].rearrange("p (a n) -> p a n", n=GROUP * D) for b in range(2)]

            def load_ids(t, b):
                sp.dma_start(src_c[:, b, :], src[:, bass.ds(t * CHUNK, CHUNK)]).then_inc(src_in[b], 16)
                sp.dma_start(dst_c[:, b, :], dst_runs[:, bass.ds(t * CHUNK, SLOTS)]).then_inc(dstc_in[b], 16)

            def load_feats(t, b):
                sp.dma_start(feat_c[:, b, :, :].rearrange("p i e -> p (i e)"), feats[bass.ds(t * P, P), :]).then_inc(feat_in[b], 16)

            def load_x(a, arrived):
                for b in range(2):
                    sp.dma_start(x_to[b][:, bass.ds(a, 1), :], x_pairs[:, b, bass.ds(a, 1), :]).then_inc(arrived[b], 16)

            load_x(0, x_first)
            load_x(1, x_next)
            for b in range(2):
                load_ids(b, b)
            with sp.Fori(0, NG // 2 - 2) as j:
                for b in range(2):
                    sp.wait_ge(x_next[b], 16 * (j + 1))
                sp.wait_ge(x_stats, 2 * j + 2)
                load_x(j + 2, x_next)

            sp.wait_ge(zeros_set, 1)
            for b in range(2):
                sp.wait_ge(table_out[b], 16 * NG // 2)

            def zero_seeds(j):
                sp.dma_start(seeds_v[:, bass.ds(j * (RUN * H // ZERO_PARTS), RUN * H // ZERO_PARTS)], zeros).then_inc(seeds_zeroed, 16)

            for j in range(ZERO_PARTS // 2):
                zero_seeds(j)
            sp.wait_ge(tgt_kept, NG)
            sp.dma_start(tgt_table_v, tgt_all[:, :, :].rearrange("p k h -> p (k h)")).then_inc(tgt_out, 16)
            sp.wait_ge(located, 1)
            sp.dma_start(fe[0:P - 1, KT:KT + 1], fe[1:P, 0:1]).then_inc(shifted, 16)
            for j in range(ZERO_PARTS // 2, ZERO_PARTS):
                zero_seeds(j)
            for b in range(2):
                load_feats(b, b)
            sp.wait_ge(nodes_placed, 1)
            sp.dma_start(first_edge_v, fe_i[:, :]).then_inc(first_out, 16)
            sp.wait_ge(run_seed_in, 16)
            for b in range(2):
                sp.wait_ge(seed_out[b], 16 * GROUP * NG // 2)
            sp.dma_start(seeds_v[:, 0:H], run_seed[:, :]).then_inc(seeds_ready, 16)
            sp.wait_ge(seeds_ready, 16)

            def store_running(t, b, before):
                sp.wait_ge(dump_ready, t + 1)
                sp.dma_start(running_v[:, bass.ds(t * (CHUNK * RW), CHUNK * RW)],
                             dump[:, b, :, :].rearrange("p c w -> p (c w)")).then_inc(dumped[b], 16)

            def load_chunk(t, b, before):
                at_least(sp, terms_ready, t - 1)
                if not isinstance(t, int) or t >= 2:
                    load_ids(t, b)
                    load_feats(t, b)
                sp.dma_start(seed_c[:, b, :, :],
                             seeds_v[:, bass.ds(t * (CHUNK * H), CHUNK * H)].rearrange("p (c h) -> p c h", h=H)).then_inc(seed_in[b], 16)

            pairwise(sp, T, load_chunk, store_running, lag=2)

            def load_x_again(g, b, before):
                at_least(sp, y_ready, g - 1)
                sp.dma_start(x_g[:, b, :, :],
                             x_v[:, bass.ds(g * (OUT_GROUP * D), OUT_GROUP * D)].rearrange("p (k d) -> p k d", k=OUT_GROUP)).then_inc(xg_in[b], 16)

            def store_y(g, b, before):
                sp.wait_ge(y_ready, g + 1)
                sp.dma_start(out_v[:, bass.ds(g * (OUT_GROUP * D), OUT_GROUP * D)],
                             y_g[:, b, :, :].rearrange("p k d -> p (k d)")).then_inc(y_out[b], 16)

            sp.wait_ge(terms_ready, T)
            pairwise(sp, NO, load_x_again, store_y, lag=2)
            sp.wait_ge(y_out[0], 16 * ((NO + 1) // 2))
            sp.wait_ge(y_out[1], 16 * (NO // 2))

        @block.gpsimd
        def _(pool):
            def gather(to, rows_of, idx):
                return pool.indirect_dma_start(to, None, rows_of, bass.IndirectOffsetOnAxis(ap=idx, axis=0))

            def scatter(rows_of, idx, values):
                return pool.indirect_dma_start(rows_of, bass.IndirectOffsetOnAxis(ap=idx, axis=0), values, None)

            pool.iota(node_i[:, :], pattern=[[1, KT + 1]], base=0, channel_multiplier=KT).then_inc(node_iota, 1)
            pool.iota(group_i[:, :, :], pattern=[[1, GROUP], [KT, P]], base=0, channel_multiplier=0).then_inc(node_iota, 1)
            pool.iota(run_spare_i[:, :], pattern=[[0, 1]], base=E, channel_multiplier=1).then_inc(node_iota, 1)
            pool.memset(ident[:, :], 0.0).then_inc(ident_zero, 1)
            pool.memset(ones[:, :], 1.0).then_inc(ones_set, 1)
            pool.wait_ge(ident_zero, 1)
            pool.affine_select(out=ident[:, :], in_=ident[:, :], compare_op=ALU.not_equal, fill=1.0, base=0,
                               pattern=[[-1, P]], channel_multiplier=1).then_inc(ident_set, 1)
            pool.memset(zeros, 0.0).then_inc(zeros_set, 1)

            def probe(s, b, before):
                at_least(pool, probed, GROUP * (s - 1))
                pool.wait_ge(piece_ready, s + 1)
                pool.sem_inc(pool_past, 1)
                for i in range(GROUP):
                    gather(probe_rows[b][:, i, :], dst, piece_i[:, b, i:i + 1]).then_inc(probe_in[b], 16)

            pairwise(pool, NG, probe)

            def place_seeds():
                pool.wait_ge(edges_in, 16)
                pool.wait_ge(tgt_out, 16)
                gather(run_seed[:, :], tgt_table, re_i[:, 0:1]).then_inc(run_seed_in, 16)
                pool.wait_ge(seeds_zeroed, 16 * ZERO_PARTS)

                def scatter_seeds(g, b, before):
                    pool.wait_ge(staged, 2 * g + 2)
                    pool.sem_inc(pool_past, 1)
                    for i in range(GROUP):
                        scatter(seeds, seed_idx[:, b, i:i + 1], seed_val[:, b, i, :]).then_inc(seed_out[b], 16)

                pairwise(pool, NG, scatter_seeds)
                pool.wait_ge(first_out, 16)
                pool.wait_ge(tail_ready, 1)
                gather(tail_end_i[:, :], first_edge, tail_next_i[:, :]).then_inc(tail_end_in, 16)

            for b in range(2):
                pool.wait_ge(table_out[b], 16 * NG // 2)

            def gather_chunk(t, b, before):
                pool.wait_ge(src_in[b], 16 * (before + 1))
                pool.sem_inc(pool_past, 1)
                for c in range(CHUNK):
                    gather(rows[:, b, c, :], table, src_c[:, b, c:c + 1]).then_inc(rows_in[b], 16)

            def gather_and_seed(t, b, before):
                gather_chunk(t, b, before)
                if isinstance(t, int) and t == 0:
                    place_seeds()

            pairwise(pool, T, gather_and_seed)

            pool.wait_ge(dumped[0], 16 * ((T + 1) // 2))
            pool.wait_ge(dumped[1], 16 * (T // 2))
            pool.wait_ge(tail_step, 3)
            gather(tail_row[:, :], running[0:E, :], tail_last_i[:, :]).then_inc(tail_row_in, 16)
            pool.wait_ge(merged_ready, 1)
            scatter(running, tail_put_i[:, :], merged[:, :]).then_inc(merged_out, 16)
            pool.wait_ge(merged_out, 16)

            def gather_last(g, b, before):
                pool.wait_ge(last_staged, g + 1)
                at_least(pool, y_ready, g - 1)
                pool.sem_inc(pool_past, 1)
                for i in range(OUT_GROUP):
                    gather(fin_rows[:, b, i, :], running[0:E, :], last_idx[:, b, i:i + 1]).then_inc(fin_in[b], 16)

            pairwise(pool, NO, gather_last)

        @block.tensor
        def _(pe):
            def sum_pieces(g, b, before):
                pe.wait_ge(compared, g + 1)
                at_least(pe, piece_ready, g)
                for i in range(GROUP):
                    for q in range(QT):
                        last = pe.matmul(banks[:, 7, i:i + 1], past[:, q, i, :], ones_b[:, :], start=(q == 0), stop=(q == QT - 1))
                last.then_inc(pieces_summed, 1)

            def turn(g, b, before):
                pe.wait_ge(x_normed, g + 1)
                at_least(pe, ht_ready, 2 * g)
                for i in range(GROUP):
                    last = pe.transpose(banks[:, 2 * b + i // 4, (i % 4) * P:(i % 4 + 1) * P], xn[:, b, i, :], ident[:, :])
                last.then_inc(transposed[b], 1)

            def project(g):
                pe.wait_ge(ht_ready, 2 * g + 2)
                at_least(pe, tab_ready, g)
                for i in range(GROUP):
                    last = pe.matmul(banks[:, 4 + i // 3, (i % 3) * RW:(i % 3 + 1) * RW], ht[:, i * P:(i + 1) * P], wc[:, :],
                                     start=True, stop=True)
                last.then_inc(projected, 1)

            def sum_and_prepare(g, b, before):
                sum_pieces(g, b, before)
                if isinstance(g, int) and g == 0:
                    pe.wait_ge(weights_in, 16 * 5)
                    pe.wait_ge(spread_a, H)
                    pe.matmul(banks[:, 5, 0:2 * H], wn[:, :], ab[:, 0:2, :].rearrange("p j h -> p (j h)"), start=True,
                              stop=True).then_inc(vectors, 1)
                    pe.matmul(banks[:, 5, 2 * H:3 * H], we2[:, :, :].rearrange("p a f -> p (a f)"), ab[:, 2, :],
                              start=True, stop=True).then_inc(vectors, 1)
                if isinstance(g, int) and g == 1:
                    pe.wait_ge(tail_diag, 1)
                    pe.wait_ge(ones_set, 1)
                    pe.matmul(banks[:, 6, 0:P], ones[:, :], diag[:, 0, :], start=True, stop=True).then_inc(tail_spread, 1)
                    pe.wait_ge(ident_set, 1)
                    pe.wait_ge(weights_ready, 3)
                    pe.wait_ge(same_ready, 1)

            def turn_and_project(g, b, before):
                if not (isinstance(g, int) and g == 0):
                    project(g - 1)
                turn(g, b, before)

            pairwise(pe, NG, sum_and_prepare, turn_and_project, more=2)
            project(NG - 1)
            pe.wait_ge(tab_ready, NG)

            def score_chunk(t, b, before):
                pe.wait_ge(feat_in[b], 16 * (before + 1))
                for i in range(PAIRS):
                    last = pe.matmul(banks[:, b, i * 2 * H:(i + 1) * 2 * H], feat_c[:, b, i, :],
                                     wscore[:, :, :].rearrange("p a h -> p (a h)"), start=True, stop=True)
                last.then_inc(scores_ready, 1)

            pairwise(pe, T, score_chunk)

            pe.wait_ge(gmax_diag, 1)
            pe.matmul(banks[:, 2, :], ones[:, :], diag[:, :, :].rearrange("p h q -> p (h q)"), start=True,
                      stop=True).then_inc(gmax_spread, 1)
            pe.wait_ge(tail_scaled, 1)
            pe.matmul(banks[:, 3, 0:W], same[:, :], tail_s[:, :, :].rearrange("p h w -> p (h w)"), start=True,
                      stop=True).then_inc(tail_sums, 1)

        @block.scalar
        def _(act):
            def count_piece(s, b, before):
                act.wait_ge(probe_in[b], 16 * GROUP * (before + 1))
                for i in range(GROUP):
                    at_least(act, probed, s * GROUP + i - 1)
                    act.activation(signs[:, (b + i) % 2, :], probe_rows[b][:, i, :], ACT.Sign,
                                   bias=half_id[:, bass.ds(s * GROUP + i, 1)], scale=-1.0,
                                   accum_out=below[:, bass.ds(s * GROUP + i, 1)]).then_inc(probed, 1)

            def deviation(g, b, before):
                act.wait_ge(x_var, g + 1)
                at_least(act, x_rstd, g - 1)
                act.activation(dev[:, b, :], var[:, :], ACT.Sqrt).then_inc(x_dev, 1)

            def relu(g, b, before):
                act.wait_ge(transposed[b], before + 1)
                at_least(act, projected, g)
                flat = banks[:, 2 * b:2 * b + 2, :].rearrange("p a n -> p (a n)")
                act.activation(ht[:, 0:4 * P], flat[:, 0:4 * P], ACT.Relu).then_inc(ht_ready, 1)
                act.activation(ht[:, 4 * P:GROUP * P], flat[:, 4 * P:GROUP * P], ACT.Relu).then_inc(ht_ready, 1)

            def take_rows(g, b, before):
                act.wait_ge(projected, g + 1)
                at_least(act, table_out[b], 16 * before)
                act.activation(tab[:, b, 0:GROUP - 1, :].rearrange("p (a i) w -> p a (i w)", i=3), banks[:, 4:6, 0:3 * RW], ACT.Copy)
                act.activation(tab[:, b, GROUP - 1, :], banks[:, 6, 0:RW], ACT.Copy).then_inc(tab_ready, 1)
                act.wait_ge(tab_ready, g + 1)
                act.activation(tgt_all[:, bass.ds(g * GROUP, GROUP), :], tab[:, b, :, W:RW], ACT.Copy).then_inc(tgt_kept, 1)
                act.dma_start(table_v[:, bass.ds(g * GROUP, GROUP), :], tab[:, b, :, 0:W]).then_inc(table_out[b], 16)

            def relu_and_count(g, b, before):
                if isinstance(g, int) and g == 0:
                    act.wait_ge(halved, 1)
                    count_piece(g, b, before)
                    relu(g, b, before)
                    take_rows(g, b, before)
                elif isinstance(g, int) and g >= NG - 2:
                    relu(g, b, before)
                    take_rows(g, b, before)
                else:
                    relu(g, b, before)
                    count_piece(g, b, before)
                    take_rows(g, b, before)

            pairwise(act, NG, deviation, relu_and_count, more=2, after=2)
            for g in range(NG - 2, NG):
                count_piece(g, g % 2, g // 2)

            act.wait_ge(nodes_placed, 3)
            act.wait_ge(tgt_kept, NG)

            def stage_seeds(g, b, before):
                at_least(act, seed_out[b], 16 * GROUP * before)
                act.activation(seed_idx[:, b, :], seed_at[:, bass.ds(g * GROUP, GROUP)], ACT.Copy).then_inc(staged, 1)
                act.activation(seed_val[:, b, :, :], tgt_all[:, bass.ds(g * GROUP, GROUP), :], ACT.Copy).then_inc(staged, 1)

            pairwise(act, NG, stage_seeds)

            def exps(t, b):
                act.wait_ge(expo_ready, t + 1)
                act.activation(expd[:, :, :, :], expo[:, :, :, :], ACT.Exp).then_inc(exps_ready, 1)

            def widen(t, b):
                act.wait_ge(fade_ready, t + 1)
                at_least(act, summed, t - 1)
                act.activation(fade_w[:, b, :, :, :], fade[:, b, :, None, :].to_broadcast([P, H, HW, SLOTS]),
                               ACT.Copy).then_inc(fade_wide, 1)

            def carry(t, b):
                act.wait_ge(summed, t)
                act.activation(terms[:, :, :, 0], sums[:, 1 - b, :, :, CHUNK], ACT.Copy).then_inc(carried, 1)

            def empty(t, b, before):
                act.wait_ge(summed, t + 1)
                at_least(act, dumped[b], 16 * before)
                act.activation(dump[:, b, :, 0:W].rearrange("p c (h w) -> p h w c", h=H), sums[:, b, :, :, 1:SLOTS], ACT.Copy)
                act.activation(dump[:, b, :, W:RW].rearrange("p c h -> p h c"), top[:, b, :, 1:SLOTS], ACT.Copy).then_inc(dump_ready, 1)

            def weights(t, b, before):
                exps(t, b)
                widen(t, b)
                if not (isinstance(t, int) and t == 0):
                    carry(t, b)

            pairwise(act, T, weights, empty)

            act.wait_ge(tail_max, 1)
            act.activation(ge[:, :, :], gd[:, :, :], ACT.Exp).then_inc(tail_scale, 1)

            def stage_last(g, b, before):
                at_least(act, fin_in[b], 16 * OUT_GROUP * before)
                act.activation(last_idx[:, b, :], last_at[:, bass.ds(g * OUT_GROUP, OUT_GROUP)], ACT.Copy).then_inc(last_staged, 1)

            def fin_exps(g, b, before):
                act.wait_ge(fin_exp_in, g + 1)
                act.activation(d1[:, :, :], fin_top[:, :, :], ACT.Exp, scale=-1.0).then_inc(fin_exp, 1)

            pairwise(act, NO, stage_last, fin_exps)

        @block.vector
        def _(dve):
            dve.wait_ge(heads_in, 16)
            dve.tensor_copy(head[:, 0, :], heads_i[:, :]).then_inc(ids_ready, 1)
            dve.memset(ones_b[:, :], 1.0)
            dve.wait_ge(node_iota, 3)
            dve.tensor_copy(group_id[:, :, :], group_i[:, :, :]).then_inc(ids_ready, 1)
            dve.wait_ge(ids_ready, 2)

            def compare(s, b, before):
                at_least(dve, heads_moved, s)
                at_least(dve, pieces_summed, s)
                for q in range(QT):
                    last = dve.tensor_scalar(past[:, q, :, :], group_id[:, :, :], head[:, b, q:q + 1], None, ALU.is_gt)
                last.then_inc(compared, 1)
                dve.tensor_scalar(head[:, 1 - b, :], head[:, b, :], -float(GROUP), None, ALU.add).then_inc(heads_moved, 1)

            def find_piece(s, b, before):
                dve.wait_ge(pieces_summed, s + 1)
                at = bass.ds(s * GROUP, GROUP)
                dve.tensor_scalar(piece[:, at], banks[:, 7, 0:GROUP], -1.0, 0.0, ALU.add, ALU.max)
                at_least(dve, probe_in[b], 16 * GROUP * before)
                dve.tensor_scalar(piece_i[:, b, :], banks[:, 7, 0:GROUP], -1.0, 0.0, ALU.add, ALU.max).then_inc(piece_ready, 1)

            step = 0

            def start_links():
                nonlocal step
                step = 0

            def link(s, ins):
                nonlocal step
                step += 1
                ins.then_inc(s, 1)
                dve.wait_ge(s, step)

            def spread_weights():
                dve.memset(ab[:, :, :], 0.0).then_inc(cleared, 1)
                dve.memset(wscore[:, :, :], 0.0).then_inc(cleared, 1)
                dve.wait_ge(cleared, 2)
                dve.wait_ge(weights_in, 16 * 5)
                for h in range(H):
                    dve.tensor_copy(ab[HD * h:HD * (h + 1), :, h], ac[HD * h:HD * (h + 1), :]).then_inc(spread_a, 1)

            def place_weights():
                dve.wait_ge(vectors, 2)
                dve.tensor_copy(wc[:, 0:W].rearrange("p (h w) -> p h w", h=H)[:, :, HD], banks[:, 5, 0:H])
                dve.tensor_copy(wc[:, W:RW], banks[:, 5, H:2 * H]).then_inc(weights_ready, 1)
                for half in range(2):
                    dve.tensor_copy(wscore[FE * half:FE * (half + 1), half, :],
                                    banks[FE * half:FE * (half + 1), 5, 2 * H:3 * H]).then_inc(weights_ready, 1)

            def find_boundaries():
                dve.tensor_copy(run_spare[:, :], run_spare_i[:, :])
                dve.tensor_copy(node_id[:, :], node_i[:, :])
                dve.tensor_scalar(half_id[:, :], node_i[:, 0:KT], -0.5, None, ALU.add).then_inc(halved, 1)
                start_links()
                dve.wait_ge(edges_in, 16)
                link(edge_step, dve.tensor_copy(re[:, :], re_i[:, :]))
                link(edge_step, dve.tensor_tensor(cont[:, :], re[:, 1:2], re[:, 2:3], ALU.is_equal))
                link(edge_step, dve.scalar_tensor_tensor(tail_id[:, :], re[:, 1:2], 1.0, cont[:, :], ALU.add, ALU.mult))
                link(edge_step, dve.tensor_scalar(tail_id[:, :], tail_id[:, :], -1.0, None, ALU.add))
                link(edge_step, dve.tensor_tensor(bt[:, 0:1], re[:, 3:4], re[:, 1:2], ALU.is_equal))
                link(edge_step, dve.tensor_tensor(bt[:, 1:2], re[:, 3:4], re[:, 4:5], ALU.is_equal))
                link(edge_step, dve.tensor_tensor(bt[:, 2:3], bt[:, 0:1], bt[:, 1:2], ALU.mult))
                link(edge_step, dve.tensor_scalar(bt[:, 3:4], bt[:, 2:3], -1.0, 1.0, ALU.mult, ALU.add))
                link(edge_step, dve.tensor_tensor(rep[:, :], bt[:, 3:4], cont[:, :], ALU.mult))
                dve.tensor_scalar(tail_next_i[:, :], re[:, 1:2], 1.0, None, ALU.add).then_inc(tail_ready, 1)
                dve.wait_ge(ident_set, 1)
                dve.tensor_scalar(diag[:, 0, :], ident[:, :], tail_id[:, 0:1], None, ALU.mult).then_inc(tail_diag, 1)
                dve.wait_ge(tail_spread, 1)
                dve.tensor_scalar(same[:, :], banks[:, 6, 0:P], tail_id[:, 0:1], None, ALU.is_equal).then_inc(same_ready, 1)

            def moments(g, b, before):
                if isinstance(g, int) and g < 2:
                    dve.wait_ge(x_first[b], 16)
                else:
                    dve.wait_ge(x_next[b], 16 * before)
                at_least(dve, x_normed, g - 1)
                for i in range(GROUP):
                    last = dve.bn_stats(st[:, i, :], x_all[b][:, bass.ds(before * (GROUP * D) + i * D, D)])
                last.then_inc(x_stats, 1)
                dve.wait_ge(x_stats, g + 1)
                dve.sem_inc(dve_past, 1)
                for i in range(GROUP):
                    last = dve.bn_aggr(mv[:, b, i, :], st[:, i, :])
                last.then_inc(x_aggr, 1)
                at_least(dve, x_dev, g)
                dve.wait_ge(x_aggr, g + 1)
                dve.tensor_scalar(var[:, :], mv[:, b, :, 1], EPS, None, ALU.add).then_inc(x_var, 1)

            def normalize(g, b, before):
                dve.wait_ge(x_dev, g + 1)
                at_least(dve, x_normed, g)
                dve.reciprocal(rstd[:, :], dev[:, b, :]).then_inc(x_rstd, 1)
                dve.wait_ge(x_rstd, g + 1)
                at_least(dve, transposed[b], before)
                for i in range(GROUP):
                    last = dve.tensor_scalar(xn[:, b, i, :], x_all[b][:, bass.ds(before * (GROUP * D) + i * D, D)],
                                             mv[:, b, i, 0:1], rstd[:, i:i + 1], ALU.subtract, ALU.mult)
                last.then_inc(x_normed, 1)

            def find_and_measure(t, b, before):
                compare(t, b, before)
                if isinstance(t, int) and t == 0:
                    spread_weights()
                    find_piece(t, b, before)
                    return
                if isinstance(t, int) and t == 1:
                    place_weights()
                    find_piece(t, b, before)
                    find_boundaries()
                    moments(0, 0, 0)
                moments(t, b, before)
                if not (isinstance(t, int) and t == 1):
                    find_piece(t, b, before)
                normalize(t - 1, 1 - b, before if b else before - 1)

            pairwise(dve, NG, find_and_measure, more=2)
            normalize(NG - 1, 1, NG // 2 - 1)

            step = 0
            link(node_step, dve.memset(fe[:, KT:KT + 1], float(E)))
            dve.wait_ge(probed, KT)
            link(node_step, dve.tensor_scalar(below[:, :], below[:, :], 0.5, HEAD / 2, ALU.mult, ALU.add))
            dve.scalar_tensor_tensor(fe[:, 0:KT], piece[:, :], float(HEAD), below[:, :], ALU.mult, ALU.add).then_inc(located, 1)
            dve.wait_ge(shifted, 16)
            link(node_step, dve.tensor_tensor(deg[:, :], fe[:, 1:KT + 1], fe[:, 0:KT], ALU.subtract))
            link(node_step, dve.tensor_scalar(some[:, :], deg[:, :], 0.0, None, ALU.is_gt))
            link(node_step, dve.tensor_scalar(none_n[:, :], deg[:, :], -1.0, float(E), ALU.mult, ALU.add))
            link(node_step, dve.tensor_scalar(spare[:, :], node_id[:, 0:KT], float(E), None, ALU.add))
            link(node_step, dve.tensor_tensor(seed_at[:, :], fe[:, 0:KT], spare[:, :], ALU.subtract))
            link(node_step, dve.tensor_tensor(seed_at[:, :], seed_at[:, :], some[:, :], ALU.mult))
            dve.tensor_copy(fe_i[:, :], fe[:, 0:KT]).then_inc(nodes_placed, 1)
            dve.tensor_tensor(seed_at[:, :], seed_at[:, :], spare[:, :], ALU.add).then_inc(nodes_placed, 1)
            dve.tensor_scalar(last_at[:, :], fe[:, 1:KT + 1], -1.0, 0.0, ALU.add, ALU.max).then_inc(nodes_placed, 1)

            dve.memset(keep[:, :, 0], 0.0)
            for b in range(2):
                dve.memset(fade[:, b, :, 0], 0.0)
                dve.memset(top[:, b, :, :], 0.0)
            dve.memset(tgt_s[:, :, CHUNK], 0.0)
            dve.wait_ge(seeds_zeroed, 16 * ZERO_PARTS)
            dve.memset(terms[:, :, :, 0], 0.0).then_inc(carries, 1)
            dve.wait_ge(carries, 1)

            def scan(dst_ap, factors, plus, combine):
                return dve.tensor_tensor_scan(dst_ap, factors, plus, 0.0, ALU.mult, combine)

            def flat(ap):
                return ap.rearrange("p h s -> p (h s)")

            def flat4(ap):
                return ap.rearrange("p h w s -> p (h w s)")

            def chunk(t, b, before):
                at_least(dve, summed, t)
                dve.wait_ge(dstc_in[b], 16 * (before + 1))
                dve.tensor_tensor(keep[:, :, 1:SLOTS], dst_c[:, b, None, 1:SLOTS].to_broadcast([P, H, CHUNK]),
                                  dst_c[:, b, None, 0:CHUNK].to_broadcast([P, H, CHUNK]), ALU.is_equal).then_inc(kept, 1)
                dve.wait_ge(seed_in[b], 16 * (before + 1))
                dve.tensor_copy(seed_s[:, :, 0], tgt_s[:, :, CHUNK])
                dve.tensor_copy(seed_s[:, :, 1:SLOTS], seed_c[:, b, :, :].rearrange("p c h -> p h c")).then_inc(seeded, 1)
                dve.wait_ge(seeded, t + 1)
                dve.wait_ge(kept, t + 1)
                scan(flat(tgt_s[:, :, :]), flat(keep[:, :, :]), flat(seed_s[:, :, :]), ALU.add).then_inc(tgt_filled, 1)
                dve.wait_ge(tgt_filled, t + 1)
                dve.wait_ge(scores_ready, t + 1)
                dve.tensor_tensor(att[:, :, :], banks[:, b, 0:CHUNK * H].rearrange("p (c h) -> p h c", h=H),
                                  tgt_s[:, :, 1:SLOTS], ALU.add).then_inc(added, 1)
                dve.wait_ge(added, t + 1)
                dve.wait_ge(rows_in[b], 16 * CHUNK * (before + 1))
                rows_h = rows[:, b, :, :].rearrange("p c (h w) -> p h w c", h=H)
                dve.tensor_tensor(att[:, :, :], att[:, :, :], rows_h[:, :, HD, :], ALU.add).then_inc(scored, 1)
                dve.wait_ge(scored, t + 1)
                dve.scalar_tensor_tensor(att[:, :, :], att[:, :, :], SLOPE, att[:, :, :], ALU.mult, ALU.max).then_inc(leaked, 1)
                dve.wait_ge(leaked, t + 1)
                dve.tensor_copy(att_s[:, :, 0], top[:, 1 - b, :, CHUNK])
                dve.tensor_scalar(att_s[:, :, 1:SLOTS], att[:, :, :], 0.0, None, ALU.max).then_inc(floored, 1)
                dve.wait_ge(floored, t + 1)
                at_least(dve, dump_ready, t - 1)
                scan(flat(top[:, b, :, :]), flat(keep[:, :, :]), flat(att_s[:, :, :]), ALU.max).then_inc(topped, 1)
                dve.wait_ge(topped, t + 1)
                dve.tensor_tensor(expo[:, 0, :, :], keep[:, :, 1:SLOTS], top[:, b, :, 0:CHUNK], ALU.mult).then_inc(faded, 1)
                dve.tensor_tensor(expo[:, 1, :, :], att[:, :, :], top[:, b, :, 1:SLOTS], ALU.subtract)
                dve.wait_ge(faded, t + 1)
                dve.tensor_tensor(expo[:, 0, :, :], expo[:, 0, :, :], top[:, b, :, 1:SLOTS], ALU.subtract).then_inc(expo_ready, 1)
                dve.memset(rows_h[:, :, HD, :], 1.0)
                dve.wait_ge(exps_ready, t + 1)
                dve.scalar_tensor_tensor(expd[:, 0, :, :], expo[:, 0, :, :], 0.0, expd[:, 0, :, :], ALU.is_ge, ALU.max).then_inc(held, 1)
                dve.wait_ge(held, t + 1)
                dve.scalar_tensor_tensor(fade[:, b, :, 1:SLOTS], expd[:, 0, :, :], 1.0, keep[:, :, 1:SLOTS], ALU.min,
                                         ALU.mult).then_inc(fade_ready, 1)
                at_least(dve, summed, t)
                dve.wait_ge(fade_ready, t + 1)
                dve.tensor_tensor(terms[:, :, :, 1:SLOTS], rows_h,
                                  expd[:, 1, :, None, :].to_broadcast([P, H, HW, CHUNK]), ALU.mult).then_inc(terms_ready, 1)
                dve.wait_ge(terms_ready, t + 1)
                dve.wait_ge(fade_wide, t + 1)
                at_least(dve, carried, t)
                at_least(dve, dump_ready, t - 1)
                scan(flat4(sums[:, b, :, :, :]), flat4(fade_w[:, b, :, :, :]), flat4(terms[:, :, :, :]), ALU.add).then_inc(summed, 1)

            pairwise(dve, T, chunk)

            dve.wait_ge(tail_end_in, 16)
            step = 0
            dve.tensor_scalar(tail_last_i[:, :], tail_end_i[:, :], -1.0, None, ALU.add)
            link(tail_step, dve.tensor_scalar(tail_end[:, :], tail_end_i[:, :], -1.0, None, ALU.add))
            link(tail_step, dve.scalar_tensor_tensor(tail_put[:, :], tail_end[:, :], run_spare[:, 0:1], rep[:, :], ALU.subtract, ALU.mult))
            link(tail_step, dve.tensor_tensor(tail_put_i[:, :], tail_put[:, :], run_spare[:, :], ALU.add))

            dve.wait_ge(topped, T)
            dve.tensor_tensor(diag[:, :, :], ident[:, None, :].to_broadcast([P, H, P]),
                              top[:, 0, :, CHUNK:SLOTS].to_broadcast([P, H, P]), ALU.mult).then_inc(gmax_diag, 1)
            dve.wait_ge(gmax_spread, 1)
            link(tail_step, dve.tensor_tensor(mask4[:, :, :], banks[:, 2, :].rearrange("p (h q) -> p h q", h=H), same[:, None, :].to_broadcast([P, H, P]), ALU.mult))
            link(tail_step, dve.tensor_reduce(gmax[:, :], mask4[:, :, :], AX_X, ALU.max))
            dve.wait_ge(tail_row_in, 16)
            link(tail_step, dve.tensor_tensor(merged[:, W:RW], gmax[:, :], tail_row[:, W:RW], ALU.max))
            dve.tensor_tensor(gd[:, 0, :], top[:, 0, :, CHUNK], merged[:, W:RW], ALU.subtract)
            dve.tensor_tensor(gd[:, 1, :], tail_row[:, W:RW], merged[:, W:RW], ALU.subtract).then_inc(tail_max, 1)
            dve.wait_ge(tail_scale, 1)
            dve.wait_ge(summed, T)
            dve.tensor_tensor(tail_s[:, :, :], sums[:, 0, :, :, CHUNK], ge[:, 0, :, None].to_broadcast([P, H, HW]),
                              ALU.mult).then_inc(tail_scaled, 1)
            row_h = tail_row[:, 0:W].rearrange("p (h w) -> p h w", h=H)
            link(tail_step, dve.tensor_tensor(row_h, row_h, ge[:, 1, :, None].to_broadcast([P, H, HW]), ALU.mult))
            dve.wait_ge(tail_sums, 1)
            dve.tensor_tensor(merged[:, 0:W], banks[:, 3, 0:W], tail_row[:, 0:W], ALU.add).then_inc(merged_ready, 1)

            def finish(g, b, before):
                dve.wait_ge(fin_in[b], 16 * OUT_GROUP * (before + 1))
                fin_h = fin_rows[:, b, :, 0:W].rearrange("p k (h w) -> p k h w", h=H)
                at = bass.ds(g * OUT_GROUP, OUT_GROUP)
                dve.tensor_copy(fin_top[:, :, :], fin_rows[:, b, :, W:RW]).then_inc(fin_exp_in, 1)
                dve.wait_ge(fin_exp, g + 1)
                dve.tensor_tensor(d2[:, :, :], d1[:, :, :], none_n[:, at, None].to_broadcast([P, OUT_GROUP, H]),
                                  ALU.mult).then_inc(fin_step, 1)
                dve.wait_ge(fin_step, 4 * g + 1)
                dve.tensor_tensor(d2[:, :, :], d2[:, :, :], fin_h[:, :, :, HD], ALU.add).then_inc(fin_step, 1)
                dve.wait_ge(fin_step, 4 * g + 2)
                dve.reciprocal(d2[:, :, :], d2[:, :, :]).then_inc(fin_step, 1)
                dve.wait_ge(fin_step, 4 * g + 3)
                dve.tensor_tensor(d2[:, :, :], d2[:, :, :], some[:, at, None].to_broadcast([P, OUT_GROUP, H]),
                                  ALU.mult).then_inc(fin_step, 1)
                dve.wait_ge(fin_step, 4 * g + 4)
                at_least(dve, y_out[b], 16 * before)
                y_h = y_g[:, b, :, :].rearrange("p k (h w) -> p k h w", h=H)
                dve.tensor_tensor(y_h, fin_h[:, :, :, 0:HD], d2[:, :, :, None].to_broadcast([P, OUT_GROUP, H, HD]),
                                  ALU.mult).then_inc(fin_free, 1)
                dve.wait_ge(fin_free, g + 1)
                dve.wait_ge(xg_in[b], 16 * (before + 1))
                dve.tensor_tensor(y_g[:, b, :, :], y_g[:, b, :, :], x_g[:, b, :, :], ALU.add).then_inc(y_ready, 1)

            pairwise(dve, NO, finish)


def kernel(**inputs):
    import numpy as np
    import concourse.bacc as bacc
    from concourse.bass_utils import run_bass_kernel_spmd

    x, src, dst = (np.asarray(inputs[n]) for n in ("x", "src", "dst"))
    feats = np.asarray(inputs["edge_attr_64"])
    w_node, w_edge, a = (np.asarray(inputs[f"L0_gnn_{n}"]) for n in ("W_node", "W_edge", "a"))
    nodes, d = x.shape
    edges, fe = feats.shape
    run = edges // P
    chunks = run // CHUNK
    heads = edges // 625
    padded = -(-nodes // (2 * GROUP * P)) * (2 * GROUP * P)
    x_rows = np.zeros((padded, d), x.dtype)
    x_rows[:nodes] = x
    dst_runs = np.full((P, run + 1), -1, dst.dtype)
    dst_runs[:, 1:] = dst.reshape(P, run)
    run_edges = np.full((P + 2, 5), -1, dst.dtype)
    run_edges[:P, 0], run_edges[:P, 1] = dst_runs[:, 1], dst_runs[:, -1]
    run_edges[:P - 1, 2:4] = run_edges[1:P, 0:2]
    run_edges[:P - 2, 4] = run_edges[2:P, 0]
    cols = np.zeros((P, chunks, SLOTS, fe), feats.dtype)
    cols[:, :, :CHUNK] = feats.reshape(P, chunks, CHUNK, fe)
    feats_t = cols.reshape(P, chunks, SLOTS // 2, 2, fe).transpose(1, 3, 4, 2, 0).reshape(chunks * 2 * fe, -1)
    n_heads, hd = a.shape[0], a.shape[1] // 3
    arrays = {
        "x": x_rows,
        "src": src.reshape(P, run),
        "dst_runs": dst_runs,
        "dst": dst.reshape(heads, -1),
        "heads": dst.reshape(heads, -1)[:, 0].reshape(-1, P).T,
        "run_edges": run_edges[:P],
        "feats": feats_t,
        "w_node": w_node,
        "w_node_t": w_node.T,
        "w_edge": w_edge,
        "a_cols": a.reshape(n_heads, 3, hd).transpose(0, 2, 1).reshape(n_heads * hd, 3),
    }
    arrays = {n: np.ascontiguousarray(v) for n, v in arrays.items()}
    nc = bacc.Bacc("TRN2", target_bir_lowering=False, num_devices=1)
    args = {n: nc.dram_tensor(f"in_{n}", v.shape, mybir.dt.from_np(v.dtype), kind="ExternalInput").ap() for n, v in arrays.items()}
    out = nc.dram_tensor("out", (padded, d), F32, kind="ExternalOutput").ap()
    gnn_kernel(nc, **args, out=out)
    r = run_bass_kernel_spmd(nc, [{f"in_{n}": v for n, v in arrays.items()}], core_ids=[0])
    return r.results[0]["out"][:nodes]
```
